# Optimizing a Trainium2 kernel written in Bass

```python
import numpy as np
import jax
import jax.numpy as jnp

def _softmax(x, axis=-1):
    return jax.nn.softmax(x, axis=axis)

def _gelu(x):
    return jax.nn.gelu(x, approximate=True)

def _silu(x):
    return jax.nn.silu(x)

def _sigmoid(x):
    return jax.nn.sigmoid(x)

def _layernorm(x, axis=-1, eps=1e-05):
    m = jnp.mean(x, axis=axis, keepdims=True)
    v = jnp.var(x, axis=axis, keepdims=True)
    return (x - m) / jnp.sqrt(v + eps)

def _scatter_add(tgt, idx, src, axis=0):
    return tgt.at[idx].add(src)

def _segment_sum(src, seg, n):
    return jax.ops.segment_sum(src, seg, n)
kernel_name = 'mk_seq_preln_d1_jaxref_r4_86093f'

def setup_inputs(seed: int=0):
    np.random.seed(seed)
    _w = jnp.asarray

    def _L0_attn_setup():
        import jax, jax.numpy as jnp
        import numpy as np
        H = 16
        G = 16
        SCALE_MIN = 0.95
        SCALE_MAX = 1.05

        def _shape_heads(x, B, S):
            return x.reshape(B, S, H, -1).transpose(0, 2, 1, 3)
        key = jax.random.key(seed)
        ks = jax.random.split(key, 9)
        B, S, E = (2, 512, 256)
        d = {'hidden_states': jax.random.normal(ks[0], (B, S, E), jnp.float32), 'Wq': jax.random.normal(ks[1], (E, E), jnp.float32) * E ** (-0.5), 'bq': jax.random.normal(ks[2], (E,), jnp.float32) * 0.02, 'Wk': jax.random.normal(ks[3], (E, E), jnp.float32) * E ** (-0.5), 'bk': jax.random.normal(ks[4], (E,), jnp.float32) * 0.02, 'Wv': jax.random.normal(ks[5], (E, E), jnp.float32) * E ** (-0.5), 'bv': jax.random.normal(ks[6], (E,), jnp.float32) * 0.02, 'Ws': jax.random.normal(ks[7], (H * G, E), jnp.float32) * E ** (-0.5), 'bs': jax.random.normal(ks[8], (H * G,), jnp.float32) * 0.02}
        return d
    _L0_attn_in = _L0_attn_setup()

    def _L0_ffn_setup():
        import jax, jax.numpy as jnp
        import numpy as np
        D_MODEL = 256
        D_FF = 1024
        NUM_EXPERTS = 8
        TOP_K = 2
        key = jax.random.key(seed)
        ks = jax.random.split(key, 8)
        s_in = 1.0 / np.sqrt(D_MODEL)
        s_ff = 1.0 / np.sqrt(D_FF)
        x = jax.random.normal(ks[0], (2, 512, D_MODEL), dtype=jnp.float32)
        Wg = jax.random.uniform(ks[1], (D_MODEL, NUM_EXPERTS), minval=-s_in, maxval=s_in, dtype=jnp.float32)
        bg = jax.random.uniform(ks[2], (NUM_EXPERTS,), minval=-s_in, maxval=s_in, dtype=jnp.float32)
        W1 = jax.random.uniform(ks[3], (NUM_EXPERTS, D_MODEL, D_FF), minval=-s_in, maxval=s_in, dtype=jnp.float32)
        b1 = jax.random.uniform(ks[4], (NUM_EXPERTS, D_FF), minval=-s_in, maxval=s_in, dtype=jnp.float32)
        W2 = jax.random.uniform(ks[5], (NUM_EXPERTS, D_FF, D_MODEL), minval=-s_ff, maxval=s_ff, dtype=jnp.float32)
        b2 = jax.random.uniform(ks[6], (NUM_EXPERTS, D_MODEL), minval=-s_ff, maxval=s_ff, dtype=jnp.float32)
        return {'x': x, 'Wg': Wg, 'bg': bg, 'W1': W1, 'b1': b1, 'W2': W2, 'b2': b2}
    _L0_ffn_in = _L0_ffn_setup()
    _d = {'L0_attn_hidden_states': _L0_attn_in['hidden_states'], 'L0_attn_Wq': _L0_attn_in['Wq'], 'L0_attn_bq': _L0_attn_in['bq'], 'L0_attn_Wk': _L0_attn_in['Wk'], 'L0_attn_bk': _L0_attn_in['bk'], 'L0_attn_Wv': _L0_attn_in['Wv'], 'L0_attn_bv': _L0_attn_in['bv'], 'L0_attn_Ws': _L0_attn_in['Ws'], 'L0_attn_bs': _L0_attn_in['bs'], 'L0_ffn_Wg': _L0_ffn_in['Wg'], 'L0_ffn_bg': _L0_ffn_in['bg'], 'L0_ffn_W1': _L0_ffn_in['W1'], 'L0_ffn_b1': _L0_ffn_in['b1'], 'L0_ffn_W2': _L0_ffn_in['W2'], 'L0_ffn_b2': _L0_ffn_in['b2']}
    _x0 = _d['L0_attn_hidden_states']
    _d['L0_attn_hidden_states'] = jax.random.normal(jax.random.fold_in(jax.random.key(seed), 1), (2, 2048, 256), dtype=_x0.dtype)
    del _x0
    return _d

def reference(L0_attn_hidden_states, L0_attn_Wq, L0_attn_bq, L0_attn_Wk, L0_attn_bk, L0_attn_Wv, L0_attn_bv, L0_attn_Ws, L0_attn_bs, L0_ffn_Wg, L0_ffn_bg, L0_ffn_W1, L0_ffn_b1, L0_ffn_W2, L0_ffn_b2):

    def _L0_attn_ref(hidden_states, Wq, bq, Wk, bk, Wv, bv, Ws, bs):
        import jax, jax.numpy as jnp
        import numpy as np
        H = 16
        G = 16
        SCALE_MIN = 0.95
        SCALE_MAX = 1.05

        def _shape_heads(x, B, S):
            return x.reshape(B, S, H, -1).transpose(0, 2, 1, 3)
        B, S, E = hidden_states.shape
        D = E // H
        gd = D // G
        Q = _shape_heads(hidden_states @ Wq.T + bq, B, S)
        K = _shape_heads(hidden_states @ Wk.T + bk, B, S)
        V = _shape_heads(hidden_states @ Wv.T + bv, B, S)
        s_logits = hidden_states @ Ws.T + bs
        s = jax.nn.sigmoid(s_logits) * (SCALE_MAX - SCALE_MIN) + SCALE_MIN
        s = s.reshape(B, S, H, G).transpose(0, 2, 1, 3)
        s = jnp.repeat(s, gd, axis=-1)
        Q = Q * s
        scores = jnp.einsum('bhsd,bhtd->bhst', Q, K) / jnp.sqrt(jnp.float32(D))
        probs = jax.nn.softmax(scores, axis=-1)
        ctx = jnp.einsum('bhst,bhtd->bhsd', probs, V)
        ctx = ctx.transpose(0, 2, 1, 3).reshape(B, S, H * D)
        return ctx

    def _L0_ffn_ref(x, Wg, bg, W1, b1, W2, b2):
        import jax, jax.numpy as jnp
        import numpy as np
        D_MODEL = 256
        D_FF = 1024
        NUM_EXPERTS = 8
        TOP_K = 2
        gate_logits = jnp.einsum('bsd,de->bse', x, Wg) + bg
        gate_probs = jax.nn.softmax(gate_logits, axis=-1)
        topk_probs, topk_idx = jax.lax.top_k(gate_probs, TOP_K)
        topk_probs = topk_probs / jnp.sum(topk_probs, axis=-1, keepdims=True)
        onehot = jax.nn.one_hot(topk_idx, NUM_EXPERTS, dtype=x.dtype)
        weights = jnp.einsum('bske,bsk->bse', onehot, topk_probs)
        h = jnp.einsum('bsd,edf->bsef', x, W1) + b1
        h = jax.nn.gelu(h, approximate=False)
        y = jnp.einsum('bsef,efd->bsed', h, W2) + b2
        return jnp.einsum('bsed,bse->bsd', y, weights)
    x = L0_attn_hidden_states
    x = x + _L0_attn_ref(_layernorm(x, axis=-1), L0_attn_Wq, L0_attn_bq, L0_attn_Wk, L0_attn_bk, L0_attn_Wv, L0_attn_bv, L0_attn_Ws, L0_attn_bs)
    x = x + _L0_ffn_ref(_layernorm(x, axis=-1), L0_ffn_Wg, L0_ffn_bg, L0_ffn_W1, L0_ffn_b1, L0_ffn_W2, L0_ffn_b2)
    return x

_drawn_inputs = setup_inputs


def setup_inputs(seed=0):
    import zlib

    import numpy as np

    out = dict(_drawn_inputs(seed))
    spreads = {}
    factors = {'L0_attn_bq': 24.344,
     'L0_attn_bk': 64.0,
     'L0_attn_Ws': 56.186,
     'L0_attn_bs': 64.0,
     'L0_ffn_b1': 6.163,
     'L0_ffn_b2': 4.334}
    for name, (base, spread) in spreads.items():
        noise = np.random.default_rng([zlib.crc32(name.encode()), seed]).standard_normal(out[name].shape)
        drawn = base * np.exp(spread * noise) if base else spread * noise
        out[name] = jnp.asarray(drawn.astype(out[name].dtype))
    for name, factor in factors.items():
        out[name] = (out[name] * factor).astype(out[name].dtype)
    return out
```

```python
import concourse.bass as bass
from concourse import mybir
from contextlib import ExitStack

B, S, E = 2, 2048, 256
H, D = 16, 16
X, F, TOP = 8, 1024, 2
P = 128
N = B * S
NT = N // P
KE, KF = E // P, F // P
CH = 512
HG = 4
DV = D + 1
ST = S // P
SC = S // CH
SLOTS = TOP * N // P + X
LN_EPS = 1e-5
S_MIN, S_RANGE = 0.95, 1.05 - 0.95
QSCALE = D ** -0.5

TERMS = [(0, 0), (0, 1), (0, 2), (1, 0), (1, 1), (2, 0)]
KROWS = len(TERMS) * D
SROWS = KROWS + 3

fp32, bf16 = mybir.dt.float32, mybir.dt.bfloat16
i32, u32 = mybir.dt.int32, mybir.dt.uint32
ALU = mybir.AluOpType
ACT = mybir.ActivationFunctionType
AX = mybir.AxisListType


def build(nc, x_in, wqT, bq, wkT, bk, wvT, bv, wsT, bs, wg, bg, w1, b1, w2, b2, out, stop=9):
    scratch = lambda name, shape, dt: nc.dram_tensor(name, shape, dt, kind="Internal").ap()
    qparts = scratch("qparts", [3, E, N], bf16)
    kparts = scratch("kparts", [3, E, N], bf16)
    mparts = scratch("mparts", [3, H, N], bf16)
    vaug = scratch("vaug", [H // HG, N, HG * DV], fp32)
    x2d = scratch("x2d", [N, E], fp32)
    xs = scratch("xs", [SLOTS * P, E], fp32)
    ys = scratch("ys", [SLOTS * P, E], fp32)

    with ExitStack() as ctx:
        sb = lambda name, shape, dt=fp32: ctx.enter_context(nc.sbuf_tensor(name, shape, dt))
        x_sb = sb("x_sb", [P, NT, E])
        w1_sb = sb("w1_sb", [P, X, KE, F])
        ident = sb("ident", [P, P])
        ones_bf = sb("ones_bf", [P, P], bf16)
        pre = ctx.enter_context(nc.semaphore("pre"))
        w1_loaded = ctx.enter_context(nc.semaphore("w1_loaded"))

        project(nc, x_sb, ident, w1_sb, w1_loaded, x_in, wqT, bq, wkT, bk, wvT, bv, wsT, bs, w1,
                qparts, kparts, vaug)
        if stop >= 2:
            row_maxima(nc, ident, qparts, kparts, mparts)
        if stop >= 3:
            attend(nc, x_sb, ident, qparts, kparts, mparts, vaug, xs)
        if stop >= 4:
            with ExitStack() as late:
                sbl = lambda name, shape, dt=fp32: late.enter_context(nc.sbuf_tensor(name, shape, dt))
                w2_sb = sbl("w2_sb", [P, X, KF, E])
                b2_sb = sbl("b2_sb", [P, X, E])
                pos, wts = sbl("pos", [P, TOP, NT], i32), sbl("wts", [P, TOP, NT])
                tile_expert = sbl("tile_expert", [1, SLOTS], i32)
                w2_loaded = late.enter_context(nc.semaphore("w2_loaded"))
                route(nc, x_sb, ident, wg, bg, x2d, xs, w1_loaded, w2_sb, w2, w2_loaded, pos, wts, tile_expert)
                b1_sb = x_sb[:, :, :].rearrange("p (x a) e -> p x (a e)", x=X)
                experts(nc, ident, w1_sb, w2_sb, b1_sb, b2_sb, b1, b2, w1_loaded, w2_loaded, tile_expert, xs, ys)
                combine(nc, x2d, ys, pos, wts, out)
        if stop <= 3:
            with ExitStack() as c2:
                o = c2.enter_context(nc.semaphore("dump"))
                blk = c2.enter_context(nc.Block())
                @blk.sync
                def _(sp):
                    sp.dma_start(out.rearrange("b (t p) e -> p (b t) e", p=P), x_sb[:, :, :]).then_inc(o, 16)
                    sp.wait_ge(w1_loaded, 16)
                    sp.wait_ge(o, 16)


def project(nc, x_sb, ident, w1_sb, w1_loaded, x_in, wqT, bq, wkT, bk, wvT, bv, wsT, bs, w1,
            qparts, kparts, vaug):
    XQ = 4
    with ExitStack() as ctx:
        sb = lambda name, shape, dt=fp32: ctx.enter_context(nc.sbuf_tensor(name, shape, dt))
        pb = lambda name, shape: ctx.enter_context(nc.psum_tensor(name, shape, fp32))
        sem = lambda name: ctx.enter_context(nc.semaphore(name))
        w_sb = sb("w_sb", [P, 4, KE, E])
        bias = sb("bias", [P, 3, KE])
        bv_sb = sb("bv_sb", [P, E])
        stats = sb("stats", [P, NT, 6])
        mean = sb("mean", [P, NT])
        rstd = sb("rstd", [P, NT])
        xn = sb("xn", [P, 2, CH // P, E])
        xnT = sb("xnT", [P, KE, CH])
        sig = sb("sig", [P, CH])
        qf = sb("qf", [P, CH])
        kf = sb("kf", [P, CH])
        qp = sb("qp", [P, KE, 3, CH], bf16)
        kp = sb("kp", [P, KE, 3, CH], bf16)
        vsb = sb("vsb", [P, 2, 2, H, DV])
        psT = pb("psT", [P, KE, CH])
        psS, psQ, psK = pb("psS", [P, CH]), pb("psQ", [P, CH]), pb("psK", [P, CH])
        psV = pb("psV", [P, 2, 2, E])

        x_loaded = [sem(f"x_loaded{i}") for i in range(XQ)]
        w_loaded, id_ready = sem("w_loaded"), sem("id_ready")
        dve_step, stats_ready, std_ready = sem("dve_step"), sem("stats_ready"), sem("std_ready")
        xn_ready, xn_free = sem("xn_ready"), sem("xn_free")
        tp_ready, xnT_ready = sem("tp_ready"), sem("xnT_ready")
        s_ready, q_ready, k_ready, v_ready = sem("s_ready"), sem("q_ready"), sem("k_ready"), sem("v_ready")
        sig_done, q_done, k_done, v_done = sem("sig_done"), sem("q_done"), sem("k_done"), sem("v_done")
        part1, rest1, part2, part3 = sem("part1"), sem("rest1"), sem("part2"), sem("part3")
        gate_step = sem("gate_step")
        parts_stored = [sem(f"parts_stored{j}") for j in range(KE)]
        v_stored = [sem(f"v_stored{i}") for i in range(2)]
        block = ctx.enter_context(nc.Block())
        NC = N // CH
        TC = CH // P

        @block.sync
        def _(sp):
            xv = x_in.rearrange("b (t p) e -> p (b t) e", p=P)
            for i in range(XQ):
                t = slice(i * NT // XQ, (i + 1) * NT // XQ)
                sp.dma_start(x_sb[:, t, :], xv[:, t, :]).then_inc(x_loaded[i], 16)
            with sp.Fori(0, NC) as c:
                for j in range(KE):
                    f = slice(j * P, (j + 1) * P)
                    sp.wait_ge(part3, 2 * KE * c + 2 * j + 2)
                    sp.dma_start(qparts[:, f, bass.ds(c * CH, CH)].rearrange("a f t -> f a t"),
                                 qp[:, j, :, :]).then_inc(parts_stored[j], 16)
                    sp.dma_start(kparts[:, f, bass.ds(c * CH, CH)].rearrange("a f t -> f a t"),
                                 kp[:, j, :, :]).then_inc(parts_stored[j], 16)
                    sp.wait_ge(v_done, 2 * c + j + 1)
                    for t in range(2):
                        sp.dma_start(vaug[:, bass.ds((c * TC + 2 * j + t) * P, P), :].rearrange("g p n -> p g n"),
                                     vsb[:, j, t, :, :].rearrange("p (g h) d -> p g (h d)", g=H // HG)
                                     ).then_inc(v_stored[j], 16)
            for j in range(KE):
                sp.wait_ge(parts_stored[j], 32 * NC)
                sp.wait_ge(v_stored[j], 32 * NC)

        @block.gpsimd
        def _(pool):
            pool.memset(ident[:, :], 0.0).then_inc(id_ready, 1)
            pool.wait_ge(id_ready, 1)
            pool.affine_select(out=ident[:, :], in_=ident[:, :], compare_op=ALU.not_equal, fill=1.0,
                               base=0, pattern=[[-1, P]], channel_multiplier=1).then_inc(id_ready, 1)

        @block.scalar
        def _(act):
            for i, w in enumerate((wqT, wkT, wsT, wvT)):
                act.dma_start(w_sb[:, i, :, :], w.rearrange("(k p) f -> p k f", p=P)).then_inc(w_loaded, 16)
            for i, b in enumerate((bq, bk, bs)):
                act.dma_start(bias[:, i, :], b.rearrange("(k p) -> p k", p=P), allow_slow_non_contiguous=True).then_inc(w_loaded, 16)
            act.dma_start(bv_sb[:, :], bv.rearrange("(a f) -> a f", a=1).broadcast_to([P, E])).then_inc(w_loaded, 16)
            act.dma_start(w1_sb[:, :, :, :], w1.rearrange("x (k p) f -> p x k f", p=P)).then_inc(w1_loaded, 16)
            act.wait_ge(stats_ready, 1)
            act.activation(rstd[:, :], rstd[:, :], ACT.Sqrt).then_inc(std_ready, 1)
            act.wait_ge(w_loaded, 16 * 8)
            with act.Fori(0, NC) as c:
                for k in range(KE):
                    act.wait_ge(tp_ready, KE * c + k + 1)
                    act.activation(xnT[:, k, :], psT[:, k, :], ACT.Copy).then_inc(xnT_ready, 1)
                for j in range(KE):
                    n = KE * c + j
                    act.wait_ge(s_ready, n + 1)
                    act.wait_ge(q_done, n)
                    act.activation(sig[:, :], psS[:, :], ACT.Sigmoid, bias=bias[:, 2, j:j + 1]).then_inc(sig_done, 1)
                    act.wait_ge(parts_stored[j], 32 * c)
                    act.wait_ge(q_done, n + 1)
                    act.activation(qp[:, j, 0, :], qf[:, :], ACT.Copy).then_inc(part1, 1)
                    act.wait_ge(k_done, n + 1)
                    act.activation(kp[:, j, 0, :], kf[:, :], ACT.Copy).then_inc(part1, 1)
                    act.wait_ge(rest1, 2 * n + 1)
                    act.activation(qp[:, j, 1, :], qf[:, :], ACT.Copy).then_inc(part2, 1)
                    act.wait_ge(rest1, 2 * n + 2)
                    act.activation(kp[:, j, 1, :], kf[:, :], ACT.Copy).then_inc(part2, 1)

        @block.tensor
        def _(pe):
            pe.wait_ge(w_loaded, 16 * 8)
            pe.wait_ge(id_ready, 2)
            with pe.Fori(0, NC // 2) as cc:
                for u in range(2):
                    c = 2 * cc + u
                    pe.wait_ge(xn_ready, c + 1)
                    for k in range(KE):
                        for t in range(TC):
                            last = nc.tensor.transpose(psT[:, k, t * P:(t + 1) * P],
                                                       xn[:, u, t, k * P:(k + 1) * P], ident[:, :])
                        last.then_inc(tp_ready, 1)
                    last = None
                    pe.wait_ge(xnT_ready, KE * c + KE)
                    for j in range(KE):
                        f = slice(j * P, (j + 1) * P)
                        n = KE * c + j
                        for w, ps, free, ready in ((2, psS, sig_done, s_ready), (0, psQ, q_done, q_ready),
                                                   (1, psK, k_done, k_ready)):
                            pe.wait_ge(free, n)
                            for k in range(KE):
                                last = nc.tensor.matmul(ps[:, :], w_sb[:, w, k, f], xnT[:, k, :],
                                                        start=k == 0, stop=k == KE - 1)
                            last.then_inc(ready, 1)
                        pe.wait_ge(v_done, 2 * c)
                        for t in range(2):
                            tile = slice((2 * j + t) * P, (2 * j + t + 1) * P)
                            for k in range(KE):
                                last = nc.tensor.matmul(psV[:, j, t, :], xnT[:, k, tile], w_sb[:, 3, k, :],
                                                        start=k == 0, stop=k == KE - 1)
                        last.then_inc(v_ready, 1)

        @block.vector
        def _(dve):
            for i in range(XQ):
                dve.wait_ge(x_loaded[i], 16)
                with dve.Fori(i * NT // XQ, (i + 1) * NT // XQ) as t:
                    nc.vector.bn_stats(stats[:, bass.ds(t, 1), :], x_sb[:, bass.ds(t, 1), :]).then_inc(dve_step, 1)
            dve.wait_ge(dve_step, NT)
            moments(nc, dve, stats, mean, rstd, dve_step, NT, stats_ready)
            nc.vector.memset(vsb[:, :, :, :, D:DV], 1.0)
            dve.wait_ge(std_ready, 1)
            nc.vector.reciprocal(rstd[:, :], rstd[:, :]).then_inc(dve_step, 1)
            dve.wait_ge(dve_step, NT + 7)

            def normalise(c, u):
                for t in range(TC):
                    tile = bass.ds(c * TC + t, 1)
                    last = nc.vector.tensor_scalar(xn[:, u, t, :], x_sb[:, tile, :].rearrange("p a e -> p (a e)"),
                                                   mean[:, tile], rstd[:, tile], ALU.subtract, ALU.mult)
                last.then_inc(xn_ready, 1)

            def chunk(c, u, more):
                for j in range(KE):
                    n = KE * c + j
                    dve.wait_ge(sig_done, n + 1)
                    nc.vector.tensor_scalar(sig[:, :], sig[:, :], S_RANGE * QSCALE, S_MIN * QSCALE,
                                            ALU.mult, ALU.add).then_inc(gate_step, 1)
                    dve.wait_ge(gate_step, n + 1)
                    dve.wait_ge(q_ready, n + 1)
                    dve.wait_ge(part3, 2 * n)
                    nc.vector.scalar_tensor_tensor(qf[:, :], psQ[:, :], bias[:, 0, j:j + 1], sig[:, :],
                                                   ALU.add, ALU.mult).then_inc(q_done, 1)
                    dve.wait_ge(k_ready, n + 1)
                    nc.vector.tensor_scalar(kf[:, :], psK[:, :], bias[:, 1, j:j + 1], None,
                                            ALU.add).then_inc(k_done, 1)
                    if j == 0 and more:
                        normalise(c + 1, 1 - u)
                    for f, (rest, parts) in enumerate(((qf, qp), (kf, kp))):
                        dve.wait_ge(part1, 2 * n + f + 1)
                        nc.vector.tensor_tensor(rest[:, :], rest[:, :], parts[:, j, 0, :],
                                                ALU.subtract).then_inc(rest1, 1)
                    for f, (rest, parts) in enumerate(((qf, qp), (kf, kp))):
                        dve.wait_ge(part2, 2 * n + f + 1)
                        nc.vector.tensor_tensor(parts[:, j, 2, :], rest[:, :], parts[:, j, 1, :],
                                                ALU.subtract).then_inc(part3, 1)
                    dve.wait_ge(v_ready, n + 1)
                    dve.wait_ge(v_stored[j], 32 * c)
                    for t in range(2):
                        last = nc.vector.tensor_tensor(vsb[:, j, t, :, 0:D],
                                                       psV[:, j, t, :].rearrange("p (h d) -> p h d", h=H),
                                                       bv_sb[:, :].rearrange("p (h d) -> p h d", h=H), ALU.add)
                    last.then_inc(v_done, 1)

            normalise(0, 0)
            with dve.Fori(0, NC // 2 - 1) as cc:
                chunk(2 * cc, 0, True)
                chunk(2 * cc + 1, 1, True)
            chunk(NC - 2, 0, True)
            chunk(NC - 1, 1, False)


def load_stacks(sp, qk, group, queries, keys, loaded, qparts, kparts, mparts=None):
    b, g = group
    for side, (stack, parts) in enumerate(((queries, qparts), (keys, kparts))):
        for r, term in enumerate(TERMS):
            sp.dma_start(stack[r * D:(r + 1) * D, :, :],
                         parts[term[side], bass.ds(g * (HG * D), HG * D), bass.ds(b * S, S)]
                         .rearrange("(h d) t -> d h t", h=HG)).then_inc(loaded, 16)
    if mparts is not None:
        sp.dma_start(queries[KROWS:SROWS, :, :],
                     mparts[:, bass.ds(g * HG, HG), bass.ds(b * S, S)]).then_inc(loaded, 16)


def row_maxima(nc, ident, qparts, kparts, mparts):
    with ExitStack() as ctx:
        sb = lambda name, shape, dt=fp32: ctx.enter_context(nc.sbuf_tensor(name, shape, dt))
        sem = lambda name: ctx.enter_context(nc.semaphore(name))
        queries = [sb(f"max_queries{i}", [KROWS, HG, S], bf16) for i in range(2)]
        keys = [sb(f"max_keys{i}", [KROWS, HG, S], bf16) for i in range(2)]
        mx = sb("mx", [P, 2, HG, ST])
        mt = sb("mt", [P, P])
        mp = sb("mp", [P, 3, P], bf16)
        ps = [ctx.enter_context(nc.psum_tensor(f"psA{i}", [P, S], fp32)) for i in range(2)]
        loaded = [sem(f"max_stacks_loaded{i}") for i in range(2)]
        scored, reduced = sem("max_scored"), sem("reduced")
        turned, m_taken, m_step, m_stored = sem("max_turned"), sem("m_taken"), sem("m_step"), sem("m_stored")
        block = ctx.enter_context(nc.Block())
        GP = H // HG // 2

        @block.sync
        def _(sp):
            with sp.Fori(0, B) as b:
                with sp.Fori(0, GP) as gp:
                    for p in range(2):
                        n = (b * GP + gp) * 2 + p
                        sp.wait_ge(turned, n + 1)
                        load_stacks(sp, None, (b, gp * 2 + p), queries[p], keys[p], loaded[p], qparts, kparts)

        @block.tensor
        def _(pe):
            pe.sem_inc(turned, 2)
            with pe.Fori(0, B) as b:
                with pe.Fori(0, GP) as gp:
                    for p in range(2):
                        n = (b * GP + gp) * 2 + p
                        with pe.Fori(0, ST) as st:
                            pe.wait_ge(loaded[p], (b * GP + gp + 1) * (16 * 2 * len(TERMS)))
                            pe.wait_ge(m_taken, n)
                            for h in range(HG):
                                i = n * (HG * ST) + st * HG + h
                                pe.wait_ge(reduced, i)
                                for c in range(S // CH):
                                    last = nc.tensor.matmul(ps[h % 2][:, c * CH:(c + 1) * CH],
                                                            queries[p][:, h, bass.ds(st * P, P)],
                                                            keys[p][:, h, c * CH:(c + 1) * CH], start=True, stop=True)
                                last.then_inc(scored, 1)
                        pe.wait_ge(reduced, (n + 1) * (HG * ST) + 1)
                        nc.tensor.transpose(ps[0][:, 0:P], mx[:, :, :, :].rearrange("p a h t -> p (a h t)"),
                                            ident[:, :]).then_inc(turned, 1)

        @block.vector
        def _(dve):
            nc.vector.memset(mx[:, :, :, :], 0.0).then_inc(reduced, 1)
            dve.wait_ge(reduced, 1)
            with dve.Fori(0, B) as b:
                with dve.Fori(0, GP) as gp:
                    for p in range(2):
                        n = (b * GP + gp) * 2 + p
                        with dve.Fori(0, ST) as st:
                            for h in range(HG):
                                dve.wait_ge(scored, n * (HG * ST) + st * HG + h + 1)
                                nc.vector.tensor_reduce(mx[:, p, h, bass.ds(st, 1)], ps[h % 2][:, :], AX.X, ALU.max,
                                                        negate=True).then_inc(reduced, 1)
                        dve.wait_ge(turned, n + 3)
                        r = slice(p * HG * ST, (p + 1) * HG * ST)
                        nc.vector.tensor_copy(mt[r, :], ps[0][r, 0:P]).then_inc(m_taken, 1)
                        dve.wait_ge(m_taken, n + 1)
                        dve.wait_ge(m_stored, n * 64)
                        for a in range(3):
                            nc.vector.tensor_copy(mp[r, a, :], mt[r, :]).then_inc(m_step, 1)
                            if a < 2:
                                dve.wait_ge(m_step, n * 5 + 2 * a + 1)
                                nc.vector.tensor_tensor(mt[r, :], mt[r, :], mp[r, a, :], ALU.subtract).then_inc(m_step, 1)
                                dve.wait_ge(m_step, n * 5 + 2 * a + 2)

        @block.scalar
        def _(act):
            with act.Fori(0, B) as b:
                with act.Fori(0, GP) as gp:
                    for p in range(2):
                        n = (b * GP + gp) * 2 + p
                        act.wait_ge(m_step, (n + 1) * 5)
                        for h in range(HG):
                            act.dma_start(mparts[:, bass.ds((gp * 2 + p) * HG + h, 1), bass.ds(b * S, S)]
                                          .rearrange("a h (t s) -> (h t) a s", s=P),
                                          mp[(p * HG + h) * ST:(p * HG + h + 1) * ST, :, :]).then_inc(m_stored, 16)
            act.wait_ge(m_stored, 64 * 2 * GP * B)


def attend(nc, x_sb, ident, qparts, kparts, mparts, vaug, xs):
    with ExitStack() as ctx:
        sb = lambda name, shape, dt=fp32: ctx.enter_context(nc.sbuf_tensor(name, shape, dt))
        pb = lambda name, shape: ctx.enter_context(nc.psum_tensor(name, shape, fp32))
        sem = lambda name: ctx.enter_context(nc.semaphore(name))
        UNITS = 2 * SC
        BLOCKS = ST * HG
        WIDE = 3
        CHUNKS = [(i, min(i + WIDE, BLOCKS)) for i in range(0, BLOCKS, WIDE)]
        NCH = len(CHUNKS)
        RING = 4
        GP = H // HG // 2
        STEPS = B * GP

        queries = [sb(f"queries{i}", [SROWS, HG, S], bf16) for i in range(2)]
        keys = [sb(f"keys{i}", [SROWS, HG, S], bf16) for i in range(2)]
        values = [sb(f"values{i}", [P, ST, HG * DV]) for i in range(2)]
        probs = sb("probs", [P, RING, WIDE, CH])
        ctxT = sb("ctxT", [P, CH])
        rec = sb("rec", [P, CH // P, HG])
        part = sb("part", [P, CH // P, HG, D])
        psP = [pb(f"psP{i}", [P, WIDE, CH]) for i in range(2)]
        psC, psM = pb("psC", [P, CH]), pb("psM", [P, CH // P, HG, 32])

        loaded = [sem(f"stacks_loaded{i}") for i in range(2)]
        v_loaded = [sem(f"values_loaded{i}") for i in range(2)]
        ones_set, stacks_free = sem("ones_set"), sem("stacks_free")
        scored, probs_ready, pv_done = sem("scored"), sem("probs_ready"), sem("pv_done")
        ctx_clear, ctx_taken, turned, added, div_step = (sem("ctx_clear"), sem("ctx_taken"), sem("turned"),
                                                         sem("added"), sem("div_step"))
        ZW = SLOTS * E // 8
        zeros = sb("zeros", [P, ZW])
        zero_set, zeroed = sem("zero_set"), sem("zeroed")
        block = ctx.enter_context(nc.Block())

        @block.sync
        def _(sp):
            with sp.Fori(0, B) as b:
                with sp.Fori(0, GP) as gp:
                    for p in range(2):
                        n = (b * GP + gp) * 2 + p
                        sp.wait_ge(stacks_free, n + 1)
                        load_stacks(sp, None, (b, gp * 2 + p), queries[p], keys[p], loaded[p],
                                    qparts, kparts, mparts)
                        sp.dma_start(values[p][:, :, :],
                                     vaug[bass.ds(gp * 2 + p, 1), bass.ds(b * S, S), :]
                                     .rearrange("g (t p) n -> p (g t) n", p=P)).then_inc(v_loaded[p], 16)

        @block.gpsimd
        def _(pool):
            for p in range(2):
                pool.memset(keys[p][KROWS:SROWS, :, :], 1.0).then_inc(ones_set, 1)
                pool.wait_ge(ones_set, p + 1)
            pool.memset(zeros[:, :], 0.0).then_inc(zero_set, 1)
            pool.wait_ge(zero_set, 1)
            with pool.Fori(0, 8) as i:
                pool.dma_start(xs[bass.ds(i * (SLOTS * P // 8), SLOTS * P // 8), :]
                               .rearrange("(p t) e -> p (t e)", p=P), zeros[:, :]).then_inc(zeroed, 16)
            pool.wait_ge(zeroed, 16 * 8)

        flat = [(u, c) for u in range(UNITS) for c in range(NCH)]

        @block.tensor
        def _(pe):
            pe.sem_inc(stacks_free, 2)
            pe.wait_ge(ones_set, 2)
            pe.wait_ge(ctx_clear, 1)

            def scores(step, n):
                u, c = flat[n]
                p, sc = u // SC, u % SC
                if sc == 0 and c == 0:
                    pe.wait_ge(loaded[p], (step + 1) * (16 * (2 * len(TERMS) + 1)))
                for i, blk in enumerate(range(*CHUNKS[c])):
                    t, h = divmod(blk, HG)
                    last = nc.tensor.matmul(psP[n % 2][:, i, :], keys[p][:, h, t * P:(t + 1) * P],
                                            queries[p][:, h, sc * CH:(sc + 1) * CH], start=True, stop=True)
                last.then_inc(scored, 1)

            def turn(step, u):
                unit = step * UNITS + u
                pe.wait_ge(added, unit)
                for t in range(CH // P):
                    last = nc.tensor.transpose(psM[:, t, :, :].rearrange("p h d -> p (h d)"),
                                               ctxT[:, t * P:(t + 1) * P], ident[:, :])
                    if t == 0 and u % SC == SC - 1:
                        last.then_inc(stacks_free, 1)
                last.then_inc(turned, 1)

            with pe.Fori(0, B) as b:
                with pe.Fori(0, GP) as gp:
                    step = b * GP + gp
                    scores(step, 0)
                    scores(step, 1)
                    for n, (u, c) in enumerate(flat):
                        p = u // SC
                        pe.wait_ge(probs_ready, step * len(flat) + n + 1)
                        if n + 2 < len(flat):
                            scores(step, n + 2)
                        before = CHUNKS[c - 1][1] // HG if c else 0
                        for t in range(before, CHUNKS[c][1] // HG):
                            if t == 0:
                                if u % SC == 0:
                                    pe.wait_ge(v_loaded[p], (step + 1) * 16)
                                pe.wait_ge(ctx_taken, step * UNITS + u)
                            for h in range(HG):
                                blk = t * HG + h
                                slot = (n - c + blk // WIDE) % RING
                                last = nc.tensor.matmul(psC[32 * h:32 * h + DV, :],
                                                        values[p][:, t, h * DV:(h + 1) * DV],
                                                        probs[:, slot, blk % WIDE, :],
                                                        start=t == 0, stop=t == ST - 1)
                            last.then_inc(pv_done, 1)
                        if c == 3 and u > 0:
                            turn(step, u - 1)
                    pe.wait_ge(ctx_taken, step * UNITS + UNITS)
                    turn(step, UNITS - 1)

        @block.scalar
        def _(act):
            with act.Fori(0, B) as b:
                with act.Fori(0, GP) as gp:
                    step = b * GP + gp
                    for n, (u, c) in enumerate(flat):
                        k = CHUNKS[c][1] - CHUNKS[c][0]
                        act.wait_ge(scored, step * len(flat) + n + 1)
                        if n >= RING:
                            uu, cc = flat[n - RING]
                            act.wait_ge(pv_done, (step * UNITS + uu) * ST + (CHUNKS[cc][1] - 1) // HG + 1)
                        elif n == 0:
                            act.wait_ge(pv_done, step * (UNITS * ST))
                        act.activation(probs[:, n % RING, 0:k, :], psP[n % 2][:, 0:k, :], ACT.Exp).then_inc(probs_ready, 1)

        @block.vector
        def _(dve):
            nc.vector.memset(psC[:, :], 0.0).then_inc(ctx_clear, 1)
            with dve.Fori(0, B) as b:
                with dve.Fori(0, GP) as gp:
                    step = b * GP + gp
                    for u in range(UNITS):
                        p, sc = u // SC, u % SC
                        unit = step * UNITS + u
                        dve.wait_ge(pv_done, (unit + 1) * ST)
                        dve.wait_ge(turned, unit)
                        nc.vector.tensor_copy(ctxT[:, :], psC[:, :]).then_inc(ctx_taken, 1)
                        dve.wait_ge(turned, unit + 1)
                        nc.vector.reciprocal(rec[:, :, :], psM[:, :, :, D]).then_inc(div_step, 1)
                        dve.wait_ge(div_step, 2 * unit + 1)
                        nc.vector.tensor_tensor(part[:, :, :, :], psM[:, :, :, 0:D],
                                                rec[:, :, :].unsqueeze(3).broadcast_to([P, CH // P, HG, D]),
                                                ALU.mult).then_inc(div_step, 1)
                        dve.wait_ge(div_step, 2 * unit + 2)
                        xs = x_sb[:, bass.ds(b * ST + sc * (CH // P), CH // P),
                                  bass.ds((gp * 2 + p) * (HG * D), HG * D)]
                        nc.vector.tensor_tensor(xs, xs, part[:, :, :, :].rearrange("p t h d -> p t (h d)"),
                                                ALU.add).then_inc(added, 1)
            dve.wait_ge(added, STEPS * UNITS)


def moments(nc, dve, stats, mean, rstd, step, base, ready):
    even, odd = stats[:, :, 1], stats[:, :, 4]
    nc.vector.tensor_tensor(mean[:, :], even, odd, ALU.add).then_inc(step, 1)
    nc.vector.tensor_tensor(rstd[:, :], stats[:, :, 2], stats[:, :, 5], ALU.add).then_inc(step, 1)
    nc.vector.tensor_tensor(stats[:, :, 0], even, odd, ALU.subtract).then_inc(step, 1)
    dve.wait_ge(step, base + 3)
    nc.vector.tensor_scalar(mean[:, :], mean[:, :], 0.5, None, ALU.mult).then_inc(step, 1)
    nc.vector.tensor_scalar(rstd[:, :], rstd[:, :], 1.0 / E, LN_EPS, ALU.mult, ALU.add).then_inc(step, 1)
    nc.vector.tensor_tensor(stats[:, :, 3], stats[:, :, 0], stats[:, :, 0], ALU.mult).then_inc(step, 1)
    dve.wait_ge(step, base + 6)
    nc.vector.scalar_tensor_tensor(rstd[:, :], stats[:, :, 3], 0.25, rstd[:, :], ALU.mult, ALU.add).then_inc(ready, 1)


def route(nc, x_sb, ident, wg, bg, x2d, xs, w1_loaded, w2_sb, w2, w2_loaded, pos, wts, tile_expert):
    with ExitStack() as ctx:
        sb = lambda name, shape, dt=fp32: ctx.enter_context(nc.sbuf_tensor("r_" + name, shape, dt))
        pb = lambda name, shape: ctx.enter_context(nc.psum_tensor("r_" + name, shape, fp32))
        sem = lambda name: ctx.enter_context(nc.semaphore("r_" + name))
        wg_sb, bg_sb = sb("wg_sb", [P, KE, X]), sb("bg_sb", [P, X])
        stats, mean, rstd = sb("stats", [P, NT, 6]), sb("mean", [P, NT]), sb("rstd", [P, NT])
        xn, xnT = sb("xn", [P, 2, E]), sb("xnT", [P, 2, KE, P])
        tri, ones = sb("tri", [P, P], bf16), sb("ones", [P, P], bf16)
        rank = sb("rank", [P, X])
        keep = sb("keep", [P, X, NT])
        slot = sb("slot", [1, SLOTS])
        logits, masked, eq = sb("logits", [P, NT, X]), sb("masked", [P, NT, X]), sb("eq", [P, NT, X])
        hot = [sb(f"hot{k}", [P, NT, X]) for k in range(TOP)]
        best = [sb(f"best{k}", [P, NT]) for k in range(TOP)]
        top, both = sb("top", [P, NT]), sb("both", [P, NT, X], bf16)
        total, upto, place = sb("total", [P, X, NT]), sb("upto", [P, X, NT]), sb("place", [P, NT, X])
        cnt_i, cnt_t = sb("cnt_i", [P, X], i32), sb("cnt_t", [P, X])
        tiles_to, base, one8 = sb("tiles_to", [P, X]), sb("base", [P, X]), sb("one8", [P, X])
        posf, past, texp = sb("posf", [P, NT]), sb("past", [1, SLOTS, X]), sb("texp", [1, SLOTS])
        psT = [pb(f"psT{i}", [P, KE, P]) for i in range(2)]
        psG, psR, psN = pb("psG", [P, NT, X]), pb("psR", [P, NT, X]), pb("psN", [P, NT, X])

        g_loaded, consts, dve_step, stats_ready, std_ready = (sem("g_loaded"), sem("consts"), sem("dve_step"),
                                                              sem("stats_ready"), sem("std_ready"))
        kept, xn_ready, tp_ready, xnT_ready, gated = (sem("kept"), sem("xn_ready"), sem("tp_ready"),
                                                      sem("xnT_ready"), sem("gated"))
        both_ready, ranked, gap_ready, exp_ready, pos_ready, scattered = (sem("both_ready"), sem("ranked"),
            sem("gap_ready"), sem("exp_ready"), sem("pos_ready"), sem("scattered"))
        block = ctx.enter_context(nc.Block())

        @block.sync
        def _(sp):
            sp.dma_start(wg_sb[:, :, :], wg.rearrange("(k p) x -> p k x", p=P)).then_inc(g_loaded, 16)
            sp.dma_start(bg_sb[:, :], bg.rearrange("(a x) -> a x", a=1).broadcast_to([P, X])).then_inc(g_loaded, 16)
            sp.dma_start(x2d.rearrange("(t p) e -> p t e", p=P), x_sb[:, :, :]).then_inc(kept, 16)
            sp.dma_start(w2_sb[:, :, :, :], w2.rearrange("x (k p) d -> p x k d", p=P)).then_inc(w2_loaded, 16)
            sp.wait_ge(kept, 16)

        @block.gpsimd
        def _(pool):
            pool.memset(tri[:, :], 1.0).then_inc(consts, 1)
            pool.memset(ones[:, :], 1.0).then_inc(consts, 1)
            pool.memset(keep[:, :, :], 1.0).then_inc(consts, 1)
            pool.memset(one8[:, :], 1.0).then_inc(consts, 1)
            pool.iota(rank[:, :], pattern=[[-1, X]], base=X, channel_multiplier=0,
                      allow_small_or_imprecise_dtypes=True).then_inc(consts, 1)
            pool.iota(slot[:, :], pattern=[[1, SLOTS]], base=0, channel_multiplier=0,
                      allow_small_or_imprecise_dtypes=True).then_inc(consts, 1)
            pool.wait_ge(consts, 6)
            pool.affine_select(out=tri[:, :], in_=tri[:, :], compare_op=ALU.is_gt, fill=0.0,
                               base=0, pattern=[[1, P]], channel_multiplier=-1).then_inc(consts, 1)
            pool.memset(keep[:, :, 0:1], 0.0).then_inc(consts, 1)
            pool.wait_ge(pos_ready, TOP)
            pool.wait_ge(xn_ready, NT)
            for k in range(TOP):
                for t in range(NT):
                    pool.indirect_dma_start(out=xs, out_offset=bass.IndirectOffsetOnAxis(ap=pos[:, k, t:t + 1], axis=0),
                                            in_=x_sb[:, t, :], in_offset=None).then_inc(scattered, 16)
            pool.wait_ge(scattered, 16 * TOP * NT)

        @block.scalar
        def _(act):
            act.wait_ge(stats_ready, 1)
            act.activation(rstd[:, :], rstd[:, :], ACT.Sqrt).then_inc(std_ready, 1)
            with act.Fori(0, NT // 2) as i:
                for u in range(2):
                    t = 2 * i + u
                    act.wait_ge(tp_ready, t + 1)
                    act.wait_ge(gated, t)
                    act.activation(xnT[:, u, :, :], psT[u][:, :, :], ACT.Copy).then_inc(xnT_ready, 1)
            act.wait_ge(gap_ready, 1)
            act.activation(top[:, :], top[:, :], ACT.Exp).then_inc(exp_ready, 1)

        @block.tensor
        def _(pe):
            pe.wait_ge(g_loaded, 32)
            with pe.Fori(0, NT // 2) as i:
                for u in range(2):
                    t = 2 * i + u
                    pe.wait_ge(xn_ready, t + 1)
                    for k in range(KE):
                        last = nc.tensor.transpose(psT[u][:, k, :], xn[:, u, k * P:(k + 1) * P], ident[:, :])
                    last.then_inc(tp_ready, 1)
                    pe.wait_ge(xnT_ready, t + 1)
                    for k in range(KE):
                        last = nc.tensor.matmul(psG[:, bass.ds(t, 1), :].rearrange("p a x -> p (a x)"), xnT[:, u, k, :],
                                                wg_sb[:, k, :], start=k == 0, stop=k == KE - 1)
                    last.then_inc(gated, 1)
            pe.wait_ge(both_ready, 1)
            pe.wait_ge(consts, 8)
            flat = both[:, :, :].rearrange("p t x -> p (t x)")
            nc.tensor.matmul(psR[:, :, :].rearrange("p t x -> p (t x)"), tri[:, :], flat, start=True, stop=True)
            nc.tensor.matmul(psN[:, :, :].rearrange("p t x -> p (t x)"), ones[:, :], flat,
                             start=True, stop=True).then_inc(ranked, 1)

        @block.vector
        def _(dve):
            with dve.Fori(0, NT) as t:
                nc.vector.bn_stats(stats[:, bass.ds(t, 1), :], x_sb[:, bass.ds(t, 1), :]).then_inc(dve_step, 1)
            dve.wait_ge(dve_step, NT)
            moments(nc, dve, stats, mean, rstd, dve_step, NT, stats_ready)
            dve.wait_ge(std_ready, 1)
            nc.vector.reciprocal(rstd[:, :], rstd[:, :]).then_inc(dve_step, 1)
            dve.wait_ge(dve_step, NT + 7)
            dve.wait_ge(kept, 16)
            with dve.Fori(0, NT // 2) as i:
                for u in range(2):
                    t = 2 * i + u
                    tile = bass.ds(t, 1)
                    dve.wait_ge(tp_ready, t)
                    src = x_sb[:, tile, :].rearrange("p a e -> p (a e)")
                    for dst in (xn[:, u, :], src):
                        last = nc.vector.tensor_scalar(dst, src, mean[:, tile], rstd[:, tile],
                                                       ALU.subtract, ALU.mult)
                    last.then_inc(xn_ready, 1)

            done = [NT + 7]

            def link(ins):
                done[0] += 1
                ins.then_inc(dve_step, 1)
                dve.wait_ge(dve_step, done[0])

            wide = lambda a: a.unsqueeze(2).broadcast_to([P, NT, X])
            each = lambda a: a.unsqueeze(1).broadcast_to([P, NT, X])
            dve.wait_ge(consts, 8)
            dve.wait_ge(gated, NT)
            link(nc.vector.tensor_tensor(logits[:, :, :], psG[:, :, :], each(bg_sb[:, :]), ALU.add))
            src = logits
            for k in range(TOP):
                link(nc.vector.tensor_reduce(best[k][:, :], src[:, :, :], AX.X, ALU.max))
                link(nc.vector.tensor_tensor(eq[:, :, :], src[:, :, :], wide(best[k][:, :]), ALU.is_equal))
                link(nc.vector.tensor_tensor(eq[:, :, :], eq[:, :, :], each(rank[:, :]), ALU.mult))
                link(nc.vector.tensor_reduce(top[:, :], eq[:, :, :], AX.X, ALU.max))
                link(nc.vector.tensor_tensor(hot[k][:, :, :], eq[:, :, :], wide(top[:, :]), ALU.is_equal))
                if k == 0:
                    link(nc.vector.scalar_tensor_tensor(masked[:, :, :], hot[0][:, :, :], -3e38, logits[:, :, :],
                                                        ALU.mult, ALU.add))
                    src = masked
            nc.vector.tensor_tensor(both[:, :, :], hot[0][:, :, :], hot[1][:, :, :], ALU.add).then_inc(both_ready, 1)
            nc.vector.tensor_tensor(top[:, :], best[1][:, :], best[0][:, :], ALU.subtract).then_inc(gap_ready, 1)
            dve.wait_ge(exp_ready, 1)
            link(nc.vector.tensor_scalar(posf[:, :], top[:, :], 1.0, None, ALU.add))
            link(nc.vector.reciprocal(wts[:, 0, :], posf[:, :]))
            link(nc.vector.tensor_tensor(wts[:, 1, :], wts[:, 0, :], top[:, :], ALU.mult))
            dve.wait_ge(ranked, 1)
            link(nc.vector.tensor_copy(total[:, :, :], psN[:, :, :].rearrange("p t x -> p x t")))
            link(nc.vector.tensor_tensor_scan(upto[:, :, :].rearrange("p x t -> p (x t)"),
                                              keep[:, :, :].rearrange("p x t -> p (x t)"),
                                              total[:, :, :].rearrange("p x t -> p (x t)"), 0.0, ALU.mult, ALU.add))
            link(nc.vector.tensor_scalar(cnt_i[:, :], upto[:, :, NT - 1], float(P - 1), None, ALU.add))
            link(nc.vector.tensor_scalar(cnt_i[:, :], cnt_i[:, :], P.bit_length() - 1, None, ALU.arith_shift_right))
            link(nc.vector.tensor_copy(cnt_t[:, :], cnt_i[:, :]))
            link(nc.vector.tensor_tensor_scan(tiles_to[:, :], one8[:, :], cnt_t[:, :], 0.0, ALU.mult, ALU.add))
            link(nc.vector.tensor_tensor(base[:, :], tiles_to[:, :], cnt_t[:, :], ALU.subtract))
            link(nc.vector.tensor_scalar(base[:, :], base[:, :], float(P), None, ALU.mult))
            link(nc.vector.tensor_tensor(upto[:, :, :], upto[:, :, :], total[:, :, :], ALU.subtract))
            link(nc.vector.tensor_tensor(place[:, :, :], psR[:, :, :], upto[:, :, :].rearrange("p x t -> p t x"), ALU.add))
            link(nc.vector.tensor_tensor(place[:, :, :], place[:, :, :], each(base[:, :]), ALU.add))
            for k in range(TOP):
                link(nc.vector.tensor_tensor(eq[:, :, :], place[:, :, :], hot[k][:, :, :], ALU.mult))
                link(nc.vector.tensor_reduce(posf[:, :], eq[:, :, :], AX.X, ALU.add))
                nc.vector.tensor_copy(pos[:, k, :], posf[:, :]).then_inc(pos_ready, 1)
                dve.wait_ge(pos_ready, k + 1)
            link(nc.vector.tensor_tensor(past[:, :, :], tiles_to[0:1, :].unsqueeze(1).broadcast_to([1, SLOTS, X]),
                                         slot[:, :].unsqueeze(2).broadcast_to([1, SLOTS, X]), ALU.is_le))
            link(nc.vector.tensor_reduce(texp[:, :], past[:, :, :], AX.X, ALU.add))
            link(nc.vector.tensor_scalar(texp[:, :], texp[:, :], float(X - 1), None, ALU.min))
            link(nc.vector.tensor_copy(tile_expert[:, :], texp[:, :]))


def experts(nc, ident, w1_sb, w2_sb, b1_sb, b2_sb, b1, b2, w1_loaded, w2_loaded, tile_expert, xs, ys):
    with ExitStack() as ctx:
        sb = lambda name, shape, dt=fp32: ctx.enter_context(nc.sbuf_tensor("e_" + name, shape, dt))
        pb = lambda name, shape: ctx.enter_context(nc.psum_tensor("e_" + name, shape, fp32))
        sem = lambda name: ctx.enter_context(nc.semaphore("e_" + name))
        xt, xT = sb("xt", [P, 2, E]), sb("xT", [P, 2, KE, P])
        h, gT, y = sb("h", [P, F]), sb("gT", [P, 2, KF, P]), sb("y", [P, 2, E])
        psX, psY = pb("psX", [P, KE, P]), pb("psY", [P, E])
        psH, psG = pb("psH", [P, 2, F // 2]), pb("psG", [P, 2, KF // 2, P])
        x_loaded = [sem(f"x_loaded{u}") for u in range(2)]
        y_stored = [sem(f"y_stored{u}") for u in range(2)]
        b_loaded = sem("b_loaded")
        x_turned, x_taken, h_ready, h_taken, g_turned, g_ready, y_ready, y_taken = (
            sem("x_turned"), sem("x_taken"), sem("h_ready"), sem("h_taken"), sem("g_turned"), sem("g_ready"),
            sem("y_ready"), sem("y_taken"))
        block = ctx.enter_context(nc.Block())

        @block.sync
        def _(sp):
            def load(j, u):
                sp.dma_start(xt[:, u, :], xs[bass.ds(j * P, P), :]).then_inc(x_loaded[u], 16)

            sp.dma_start(b1_sb, b1.rearrange("(a x) f -> a x f", a=1).broadcast_to([P, X, F])).then_inc(b_loaded, 16)
            sp.dma_start(b2_sb[:, :, :], b2.rearrange("(a x) f -> a x f", a=1).broadcast_to([P, X, E])).then_inc(b_loaded, 16)
            load(0, 0)
            load(1, 1)
            with sp.Fori(0, SLOTS // 2 - 1) as i:
                for u in range(2):
                    sp.wait_ge(x_turned, 2 * i + u + 1)
                    load(2 * i + 2 + u, u)

        @block.tensor
        def _(pe):
            pe.wait_ge(w1_loaded, 16)

            def expert(j):
                return pe.value_load(tile_expert[0:1, bass.ds(j, 1)], min_val=0, max_val=X - 1)

            def turn_x(j, u, i):
                pe.wait_ge(x_loaded[u], 16 * (i + 1))
                pe.wait_ge(x_taken, j)
                for k in range(KE):
                    last = nc.tensor.transpose(psX[:, k, :], xt[:, u, k * P:(k + 1) * P], ident[:, :])
                last.then_inc(x_turned, 1)

            def up(j, u, e):
                pe.wait_ge(x_taken, j + 1)
                pe.wait_ge(h_taken, 2 * j)
                for c in range(2):
                    for k in range(KE):
                        last = nc.tensor.matmul(psH[:, c, :], xT[:, u, k, :],
                                                w1_sb[:, bass.ds(e, 1), k, c * (F // 2):(c + 1) * (F // 2)]
                                                .rearrange("p a f -> p (a f)"), start=k == 0, stop=k == KE - 1)
                    last.then_inc(h_ready, 1)

            def turn_h(j):
                for c in range(2):
                    pe.wait_ge(h_taken, 2 * j + c + 1)
                    pe.wait_ge(g_ready, 2 * j)
                    for k in range(KF // 2):
                        f = c * (F // 2) + k * P
                        last = nc.tensor.transpose(psG[:, c, k, :], h[:, f:f + P], ident[:, :])
                    last.then_inc(g_turned, 1)

            def down(j, u, e):
                pe.wait_ge(g_ready, 2 * j + 2)
                pe.wait_ge(y_taken, j)
                for k in range(KF):
                    last = nc.tensor.matmul(psY[:, :], gT[:, u, k, :],
                                            w2_sb[:, bass.ds(e, 1), k, :].rearrange("p a f -> p (a f)"),
                                            start=k == 0, stop=k == KF - 1)
                last.then_inc(y_ready, 1)

            turn_x(0, 0, 0)
            up(0, 0, expert(0))
            turn_x(1, 1, 0)
            turn_h(0)
            pe.wait_ge(w2_loaded, 16)
            with pe.Fori(0, SLOTS // 2 - 1) as i:
                for v in range(2):
                    j, u = 2 * i + 1 + v, 1 - v
                    up(j, u, expert(j))
                    turn_x(j + 1, 1 - u, i + 1)
                    down(j - 1, 1 - u, expert(j - 1))
                    turn_h(j)
            up(SLOTS - 1, 1, expert(SLOTS - 1))
            down(SLOTS - 2, 0, expert(SLOTS - 2))
            turn_h(SLOTS - 1)
            down(SLOTS - 1, 1, expert(SLOTS - 1))

        @block.vector
        def _(dve):
            dve.wait_ge(b_loaded, 32)

            def expert(j):
                return dve.value_load(tile_expert[0:1, bass.ds(j, 1)], min_val=0, max_val=X - 1)

            def take_x(j, u):
                dve.wait_ge(x_turned, j + 1)
                nc.vector.tensor_copy(xT[:, u, :, :], psX[:, :, :]).then_inc(x_taken, 1)

            def take_h(j, e):
                for c in range(2):
                    dve.wait_ge(h_ready, 2 * j + c + 1)
                    dve.wait_ge(g_turned, 2 * j)
                    half = slice(c * (F // 2), (c + 1) * (F // 2))
                    nc.vector.tensor_tensor(h[:, half], psH[:, c, :],
                                            b1_sb[:, bass.ds(e, 1), half].rearrange("p a f -> p (a f)"),
                                            ALU.add).then_inc(h_taken, 1)

            def take_y(j, u, i, e):
                dve.wait_ge(y_ready, j + 1)
                dve.wait_ge(y_stored[u], 16 * i)
                nc.vector.tensor_tensor(y[:, u, :], psY[:, :],
                                        b2_sb[:, bass.ds(e, 1), :].rearrange("p a f -> p (a f)"),
                                        ALU.add).then_inc(y_taken, 1)

            take_x(0, 0)
            take_h(0, expert(0))
            take_x(1, 1)
            with dve.Fori(0, SLOTS // 2 - 1) as i:
                for v in range(2):
                    j, u = 2 * i + 1 + v, 1 - v
                    take_h(j, expert(j))
                    take_x(j + 1, 1 - u)
                    take_y(j - 1, 1 - u, i, expert(j - 1))
            take_h(SLOTS - 1, expert(SLOTS - 1))
            take_y(SLOTS - 2, 0, SLOTS // 2 - 1, expert(SLOTS - 2))
            take_y(SLOTS - 1, 1, SLOTS // 2 - 1, expert(SLOTS - 1))

        @block.scalar
        def _(act):
            with act.Fori(0, SLOTS // 2) as i:
                for u in range(2):
                    j = 2 * i + u
                    for c in range(2):
                        act.wait_ge(g_turned, 2 * j + c + 1)
                        act.activation(gT[:, u, c * (KF // 2):(c + 1) * (KF // 2), :], psG[:, c, :, :],
                                       ACT.Gelu).then_inc(g_ready, 1)

        @block.gpsimd
        def _(pool):
            with pool.Fori(0, SLOTS // 2) as i:
                for u in range(2):
                    pool.wait_ge(y_taken, 2 * i + u + 1)
                    pool.dma_start(ys[bass.ds((2 * i + u) * P, P), :], y[:, u, :]).then_inc(y_stored[u], 16)
            for u in range(2):
                pool.wait_ge(y_stored[u], 16 * (SLOTS // 2))


def combine(nc, x2d, ys, pos, wts, out):
    with ExitStack() as ctx:
        sb = lambda name, shape, dt=fp32: ctx.enter_context(nc.sbuf_tensor("c_" + name, shape, dt))
        sem = lambda name: ctx.enter_context(nc.semaphore("c_" + name))
        RING = 4
        xr, yr, r = sb("xr", [P, RING, E]), sb("yr", [P, RING, TOP, E]), sb("r", [P, RING, E])
        x_loaded = [sem(f"x_loaded{i}") for i in range(RING)]
        gathered = [sem(f"gathered{i}") for i in range(RING)]
        stored = [sem(f"stored{i}") for i in range(RING)]
        half, summed = sem("half"), sem("summed")
        block = ctx.enter_context(nc.Block())
        ov = out.rearrange("b s e -> (b s) e")

        @block.gpsimd
        def _(pool):
            for t in range(NT):
                if t >= RING:
                    pool.wait_ge(summed, t - RING + 1)
                for k in range(TOP):
                    pool.indirect_dma_start(out=yr[:, t % RING, k, :], out_offset=None, in_=ys,
                                            in_offset=bass.IndirectOffsetOnAxis(ap=pos[:, k, t:t + 1], axis=0)
                                            ).then_inc(gathered[t % RING], 16)

        @block.scalar
        def _(act):
            for t in range(NT):
                if t >= RING:
                    act.wait_ge(summed, t - RING + 1)
                act.dma_start(xr[:, t % RING, :], x2d[t * P:(t + 1) * P, :]).then_inc(x_loaded[t % RING], 16)

        @block.vector
        def _(dve):
            for t in range(NT):
                i, n = t % RING, t // RING
                dve.wait_ge(x_loaded[i], 16 * (n + 1))
                dve.wait_ge(gathered[i], 32 * (n + 1))
                if n:
                    dve.wait_ge(stored[i], 16 * n)
                nc.vector.scalar_tensor_tensor(r[:, i, :], yr[:, i, 0, :], wts[:, 0, t:t + 1], xr[:, i, :],
                                               ALU.mult, ALU.add).then_inc(half, 1)
                dve.wait_ge(half, t + 1)
                nc.vector.scalar_tensor_tensor(r[:, i, :], yr[:, i, 1, :], wts[:, 1, t:t + 1], r[:, i, :],
                                               ALU.mult, ALU.add).then_inc(summed, 1)

        @block.sync
        def _(sp):
            for t in range(NT):
                sp.wait_ge(summed, t + 1)
                sp.dma_start(ov[t * P:(t + 1) * P, :], r[:, t % RING, :]).then_inc(stored[t % RING], 16)
            for i in range(RING):
                sp.wait_ge(stored[i], 16 * (NT // RING))


_OUT = "out_dram"


def kernel(**inputs):
    import numpy as _np
    import concourse.bacc as _bacc
    from concourse import mybir as _mybir
    from concourse.bass_utils import run_bass_kernel_spmd as _run

    get = {k: _np.asarray(v) for k, v in inputs.items()}
    a, f = "L0_attn_", "L0_ffn_"
    order = [("x", get[a + "hidden_states"])]
    for w in ("q", "k", "v", "s"):
        order.append((f"w{w}T", get[a + "W" + w].T))
        order.append((f"b{w}", get[a + "b" + w]))
    order += [(n.lower(), get[f + n]) for n in ("Wg", "bg", "W1", "b1", "W2", "b2")]
    nc = _bacc.Bacc("TRN2", target_bir_lowering=False, num_devices=1)
    arrays, args = {}, []
    for name, v in order:
        arrays[name] = _np.ascontiguousarray(v)
        args.append(nc.dram_tensor(name, v.shape, _mybir.dt.from_np(v.dtype), kind="ExternalInput").ap())
    args.append(nc.dram_tensor(_OUT, (B, S, E), _mybir.dt.from_np(_np.dtype("float32")), kind="ExternalOutput").ap())
    build(nc, *args)
    return _run(nc, [arrays], core_ids=[0]).results[0][_OUT]
```

```python
import concourse.bass as bass
from concourse import mybir
from contextlib import ExitStack

B, S, E = 2, 2048, 256
H, D = 16, 16
X, F, TOP = 8, 1024, 2
P = 128
N = B * S
NT = N // P
KE, KF = E // P, F // P
CH = 512
HG = 4
DV = D + 1
ST = S // P
SC = S // CH
SLOTS = TOP * N // P + X
LN_EPS = 1e-5
S_MIN, S_RANGE = 0.95, 1.05 - 0.95
QSCALE = D ** -0.5

TERMS = [(0, 0), (0, 1), (0, 2), (1, 0), (1, 1), (2, 0)]
KROWS = len(TERMS) * D
SROWS = KROWS + 3

fp32, bf16 = mybir.dt.float32, mybir.dt.bfloat16
i32, u32 = mybir.dt.int32, mybir.dt.uint32
ALU = mybir.AluOpType
ACT = mybir.ActivationFunctionType
AX = mybir.AxisListType


def build(nc, x_in, wqT, bq, wkT, bk, wvT, bv, wsT, bs, wg, bg, w1, b1, w2, b2, out, stop=9):
    scratch = lambda name, shape, dt: nc.dram_tensor(name, shape, dt, kind="Internal").ap()
    qparts = scratch("qparts", [3, B * E, S], bf16)
    kparts = scratch("kparts", [3, B * E, S], bf16)
    mparts = scratch("mparts", [B * H // HG, SC, 3, HG * CH // P, P], bf16)
    vaug = scratch("vaug", [B * H // HG, S, HG * DV], fp32)
    x2d = scratch("x2d", [N, E], fp32)
    xs = scratch("xs", [SLOTS * P, E], fp32)
    ys = scratch("ys", [SLOTS * P, E], fp32)

    with ExitStack() as ctx:
        sb = lambda name, shape, dt=fp32: ctx.enter_context(nc.sbuf_tensor(name, shape, dt))
        x_sb = sb("x_sb", [P, NT, E])
        w1_sb = sb("w1_sb", [P, X, KE, F])
        ident = sb("ident", [P, P])
        ones_bf = sb("ones_bf", [P, P], bf16)
        pre = ctx.enter_context(nc.semaphore("pre"))
        w1_loaded = ctx.enter_context(nc.semaphore("w1_loaded"))

        project(nc, x_sb, ident, w1_sb, w1_loaded, x_in, wqT, bq, wkT, bk, wvT, bv, wsT, bs, w1,
                qparts, kparts, vaug)
        if stop >= 3:
            attend(nc, x_sb, ident, qparts, kparts, mparts, vaug, xs)
        if stop >= 4:
            with ExitStack() as late:
                sbl = lambda name, shape, dt=fp32: late.enter_context(nc.sbuf_tensor(name, shape, dt))
                w2_sb = sbl("w2_sb", [P, X, KF, E])
                b2_sb = sbl("b2_sb", [P, X, E])
                pos, wts = sbl("pos", [P, TOP, NT], i32), sbl("wts", [P, TOP, NT])
                tile_expert = sbl("tile_expert", [1, SLOTS], i32)
                w2_loaded = late.enter_context(nc.semaphore("w2_loaded"))
                route(nc, x_sb, ident, wg, bg, x2d, xs, w1_loaded, w2_sb, w2, w2_loaded, pos, wts, tile_expert)
                b1_sb = x_sb[:, :, :].rearrange("p (x a) e -> p x (a e)", x=X)
                experts(nc, ident, w1_sb, w2_sb, b1_sb, b2_sb, b1, b2, w1_loaded, w2_loaded, tile_expert, xs, ys)
                combine(nc, x2d, ys, pos, wts, out)
        if stop <= 3:
            with ExitStack() as c2:
                o = c2.enter_context(nc.semaphore("dump"))
                blk = c2.enter_context(nc.Block())
                @blk.sync
                def _(sp):
                    sp.dma_start(out.rearrange("b (t p) e -> p (b t) e", p=P), x_sb[:, :, :]).then_inc(o, 16)
                    sp.wait_ge(w1_loaded, 16)
                    sp.wait_ge(o, 16)


def project(nc, x_sb, ident, w1_sb, w1_loaded, x_in, wqT, bq, wkT, bk, wvT, bv, wsT, bs, w1,
            qparts, kparts, vaug):
    XQ = 4
    with ExitStack() as ctx:
        sb = lambda name, shape, dt=fp32: ctx.enter_context(nc.sbuf_tensor(name, shape, dt))
        pb = lambda name, shape: ctx.enter_context(nc.psum_tensor(name, shape, fp32))
        sem = lambda name: ctx.enter_context(nc.semaphore(name))
        w_sb = sb("w_sb", [P, 4, KE, E])
        bias = sb("bias", [P, 3, KE])
        bv_sb = sb("bv_sb", [P, E])
        stats = sb("stats", [P, NT, 6])
        mean = sb("mean", [P, NT])
        rstd = sb("rstd", [P, NT])
        xn = sb("xn", [P, 2, CH // P, E])
        xnT = sb("xnT", [P, KE, CH])
        sig = sb("sig", [P, CH])
        qf = sb("qf", [P, CH])
        kf = sb("kf", [P, CH])
        qp = sb("qp", [P, KE, 3, CH], bf16)
        kp = sb("kp", [P, KE, 3, CH], bf16)
        vsb = sb("vsb", [P, 2, 2, H, DV])
        psT = pb("psT", [P, KE, CH])
        psS, psQ, psK = pb("psS", [P, CH]), pb("psQ", [P, CH]), pb("psK", [P, CH])
        psV = pb("psV", [P, 2, 2, E])

        x_loaded = [sem(f"x_loaded{i}") for i in range(XQ)]
        w_loaded, id_ready = sem("w_loaded"), sem("id_ready")
        dve_step, stats_ready, std_ready = sem("dve_step"), sem("stats_ready"), sem("std_ready")
        xn_ready, xn_free = sem("xn_ready"), sem("xn_free")
        tp_ready, xnT_ready = sem("tp_ready"), sem("xnT_ready")
        s_ready, q_ready, k_ready, v_ready = sem("s_ready"), sem("q_ready"), sem("k_ready"), sem("v_ready")
        sig_done, q_done, k_done, v_done = sem("sig_done"), sem("q_done"), sem("k_done"), sem("v_done")
        part1, rest1, part2, part3 = sem("part1"), sem("rest1"), sem("part2"), sem("part3")
        gate_step = sem("gate_step")
        parts_stored = [sem(f"parts_stored{j}") for j in range(KE)]
        v_stored = [sem(f"v_stored{i}") for i in range(2)]
        block = ctx.enter_context(nc.Block())
        NC = N // CH
        TC = CH // P

        @block.sync
        def _(sp):
            xv = x_in.rearrange("b (t p) e -> p (b t) e", p=P)
            for i in range(XQ):
                t = slice(i * NT // XQ, (i + 1) * NT // XQ)
                sp.dma_start(x_sb[:, t, :], xv[:, t, :]).then_inc(x_loaded[i], 16)
            with sp.Fori(0, B) as b:
                with sp.Fori(0, SC) as sc:
                    c = b * SC + sc
                    for j in range(KE):
                        f = bass.ds(b * E + j * P, P)
                        sp.wait_ge(part3, 2 * KE * c + 2 * j + 2)
                        for dst, src in ((qparts, qp), (kparts, kp)):
                            sp.dma_start(dst[:, f, bass.ds(sc * CH, CH)].rearrange("a f t -> f a t"),
                                         src[:, j, :, :]).then_inc(parts_stored[j], 16)
                        sp.wait_ge(v_done, 2 * c + j + 1)
                        for t in range(2):
                            sp.dma_start(vaug[bass.ds(b * (H // HG), H // HG),
                                              bass.ds((sc * TC + 2 * j + t) * P, P), :].rearrange("g p n -> p g n"),
                                         vsb[:, j, t, :, :].rearrange("p (g h) d -> p g (h d)", g=H // HG)
                                         ).then_inc(v_stored[j], 16)
            for j in range(KE):
                sp.wait_ge(parts_stored[j], 32 * NC)
                sp.wait_ge(v_stored[j], 32 * NC)

        @block.gpsimd
        def _(pool):
            pool.memset(ident[:, :], 0.0).then_inc(id_ready, 1)
            pool.wait_ge(id_ready, 1)
            pool.affine_select(out=ident[:, :], in_=ident[:, :], compare_op=ALU.not_equal, fill=1.0,
                               base=0, pattern=[[-1, P]], channel_multiplier=1).then_inc(id_ready, 1)

        @block.scalar
        def _(act):
            for i, w in enumerate((wqT, wkT, wsT, wvT)):
                act.dma_start(w_sb[:, i, :, :], w.rearrange("(k p) f -> p k f", p=P)).then_inc(w_loaded, 16)
            for i, b in enumerate((bq, bk, bs)):
                act.dma_start(bias[:, i, :], b.rearrange("(k p) -> p k", p=P), allow_slow_non_contiguous=True).then_inc(w_loaded, 16)
            act.dma_start(bv_sb[:, :], bv.rearrange("(a f) -> a f", a=1).broadcast_to([P, E])).then_inc(w_loaded, 16)
            act.dma_start(w1_sb[:, :, :, :], w1.rearrange("x (k p) f -> p x k f", p=P)).then_inc(w1_loaded, 16)
            act.wait_ge(stats_ready, 1)
            act.activation(rstd[:, :], rstd[:, :], ACT.Sqrt).then_inc(std_ready, 1)
            act.wait_ge(w_loaded, 16 * 8)
            with act.Fori(0, NC) as c:
                for k in range(KE):
                    act.wait_ge(tp_ready, KE * c + k + 1)
                    act.activation(xnT[:, k, :], psT[:, k, :], ACT.Copy).then_inc(xnT_ready, 1)
                for j in range(KE):
                    n = KE * c + j
                    act.wait_ge(s_ready, n + 1)
                    act.wait_ge(q_done, n)
                    act.activation(sig[:, :], psS[:, :], ACT.Sigmoid, bias=bias[:, 2, j:j + 1]).then_inc(sig_done, 1)
                    act.wait_ge(parts_stored[j], 32 * c)
                    act.wait_ge(q_done, n + 1)
                    act.activation(qp[:, j, 0, :], qf[:, :], ACT.Copy).then_inc(part1, 1)
                    act.wait_ge(k_done, n + 1)
                    act.activation(kp[:, j, 0, :], kf[:, :], ACT.Copy).then_inc(part1, 1)
                    act.wait_ge(rest1, 2 * n + 1)
                    act.activation(qp[:, j, 1, :], qf[:, :], ACT.Copy).then_inc(part2, 1)
                    act.wait_ge(rest1, 2 * n + 2)
                    act.activation(kp[:, j, 1, :], kf[:, :], ACT.Copy).then_inc(part2, 1)

        @block.tensor
        def _(pe):
            pe.wait_ge(w_loaded, 16 * 8)
            pe.wait_ge(id_ready, 2)
            with pe.Fori(0, NC // 2) as cc:
                for u in range(2):
                    c = 2 * cc + u
                    pe.wait_ge(xn_ready, c + 1)
                    for k in range(KE):
                        for t in range(TC):
                            last = nc.tensor.transpose(psT[:, k, t * P:(t + 1) * P],
                                                       xn[:, u, t, k * P:(k + 1) * P], ident[:, :])
                        last.then_inc(tp_ready, 1)
                    last = None
                    pe.wait_ge(xnT_ready, KE * c + KE)
                    for j in range(KE):
                        f = slice(j * P, (j + 1) * P)
                        n = KE * c + j
                        for w, ps, free, ready in ((2, psS, sig_done, s_ready), (0, psQ, q_done, q_ready),
                                                   (1, psK, k_done, k_ready)):
                            pe.wait_ge(free, n)
                            for k in range(KE):
                                last = nc.tensor.matmul(ps[:, :], w_sb[:, w, k, f], xnT[:, k, :],
                                                        start=k == 0, stop=k == KE - 1)
                            last.then_inc(ready, 1)
                        pe.wait_ge(v_done, 2 * c)
                        for t in range(2):
                            tile = slice((2 * j + t) * P, (2 * j + t + 1) * P)
                            for k in range(KE):
                                last = nc.tensor.matmul(psV[:, j, t, :], xnT[:, k, tile], w_sb[:, 3, k, :],
                                                        start=k == 0, stop=k == KE - 1)
                        last.then_inc(v_ready, 1)

        @block.vector
        def _(dve):
            for i in range(XQ):
                dve.wait_ge(x_loaded[i], 16)
                with dve.Fori(i * NT // XQ, (i + 1) * NT // XQ) as t:
                    nc.vector.bn_stats(stats[:, bass.ds(t, 1), :], x_sb[:, bass.ds(t, 1), :]).then_inc(dve_step, 1)
            dve.wait_ge(dve_step, NT)
            moments(nc, dve, stats, mean, rstd, dve_step, NT, stats_ready)
            nc.vector.memset(vsb[:, :, :, :, D:DV], 1.0)
            dve.wait_ge(std_ready, 1)
            nc.vector.reciprocal(rstd[:, :], rstd[:, :]).then_inc(dve_step, 1)
            dve.wait_ge(dve_step, NT + 7)

            def normalise(c, u):
                for t in range(TC):
                    tile = bass.ds(c * TC + t, 1)
                    last = nc.vector.tensor_scalar(xn[:, u, t, :], x_sb[:, tile, :].rearrange("p a e -> p (a e)"),
                                                   mean[:, tile], rstd[:, tile], ALU.subtract, ALU.mult)
                last.then_inc(xn_ready, 1)

            def chunk(c, u, more):
                for j in range(KE):
                    n = KE * c + j
                    dve.wait_ge(sig_done, n + 1)
                    nc.vector.tensor_scalar(sig[:, :], sig[:, :], S_RANGE * QSCALE, S_MIN * QSCALE,
                                            ALU.mult, ALU.add).then_inc(gate_step, 1)
                    dve.wait_ge(gate_step, n + 1)
                    dve.wait_ge(q_ready, n + 1)
                    dve.wait_ge(part3, 2 * n)
                    nc.vector.scalar_tensor_tensor(qf[:, :], psQ[:, :], bias[:, 0, j:j + 1], sig[:, :],
                                                   ALU.add, ALU.mult).then_inc(q_done, 1)
                    dve.wait_ge(k_ready, n + 1)
                    nc.vector.tensor_scalar(kf[:, :], psK[:, :], bias[:, 1, j:j + 1], None,
                                            ALU.add).then_inc(k_done, 1)
                    if j == 0 and more:
                        normalise(c + 1, 1 - u)
                    for f, (rest, parts) in enumerate(((qf, qp), (kf, kp))):
                        dve.wait_ge(part1, 2 * n + f + 1)
                        nc.vector.tensor_tensor(rest[:, :], rest[:, :], parts[:, j, 0, :],
                                                ALU.subtract).then_inc(rest1, 1)
                    for f, (rest, parts) in enumerate(((qf, qp), (kf, kp))):
                        dve.wait_ge(part2, 2 * n + f + 1)
                        nc.vector.tensor_tensor(parts[:, j, 2, :], rest[:, :], parts[:, j, 1, :],
                                                ALU.subtract).then_inc(part3, 1)
                    dve.wait_ge(v_ready, n + 1)
                    dve.wait_ge(v_stored[j], 32 * c)
                    for t in range(2):
                        last = nc.vector.tensor_tensor(vsb[:, j, t, :, 0:D],
                                                       psV[:, j, t, :].rearrange("p (h d) -> p h d", h=H),
                                                       bv_sb[:, :].rearrange("p (h d) -> p h d", h=H), ALU.add)
                    last.then_inc(v_done, 1)

            normalise(0, 0)
            with dve.Fori(0, NC // 2 - 1) as cc:
                chunk(2 * cc, 0, True)
                chunk(2 * cc + 1, 1, True)
            chunk(NC - 2, 0, True)
            chunk(NC - 1, 1, False)


def rewind(nc, sems):
    nc.gpsimd.sem_clear(range(sems[0].num, sems[-1].num + 1))
    nc.all_engine_barrier()


def attend(nc, x_sb, ident, qparts, kparts, mparts, vaug, xs):
    with ExitStack() as ctx:
        sb = lambda name, shape, dt=fp32: ctx.enter_context(nc.sbuf_tensor("a_" + name, shape, dt))
        pb = lambda name, shape: ctx.enter_context(nc.psum_tensor("a_" + name, shape, fp32))
        UNITS = 2 * SC
        BLOCKS = ST * HG
        RING = 3 * HG
        QT = CH // P
        AHEAD = 2
        GROUPS = B * H // HG
        STACK_DMAS = 16 * 2 * len(TERMS)

        queries = [sb(f"queries{i}", [SROWS, HG, S], bf16) for i in range(2)]
        keys = [sb(f"keys{i}", [SROWS, HG, S], bf16) for i in range(2)]
        values = [sb(f"values{i}", [P, ST, HG * DV]) for i in range(2)]
        probs = sb("probs", [P, RING, CH])
        ctxT = sb("ctxT", [P, CH])
        rec = sb("rec", [P, QT, HG])
        part = sb("part", [P, QT, HG, D])
        halfmax = sb("halfmax", [P, 2, HG * QT])
        negmax = sb("negmax", [P, 2, HG * QT])
        mt = sb("mt", [HG * QT, P])
        mp = sb("mp", [HG * QT, 2, 3, P], bf16)
        zeros = sb("zeros", [P, SLOTS * E // 8])
        psA = [pb(f"psA{i}", [P, S // 2]) for i in range(2)]
        psP = [pb(f"psP{i}", [P, CH]) for i in range(2)]
        psC, psM = pb("psC", [P, CH]), pb("psM", [P, QT, HG, 32])
        turned_max = psM[0:HG * QT, :, :, :].rearrange("p t h d -> p (t h d)")[:, 0:P]

        sems = []

        def sem(name):
            sems.append(ctx.enter_context(nc.semaphore("a_" + name)))
            return sems[-1]

        loaded = [sem(f"stacks_loaded{i}") for i in range(2)]
        v_loaded = [sem(f"values_loaded{i}") for i in range(2)]
        ones_set, zero_set, zeroed, ctx_clear = sem("ones_set"), sem("zero_set"), sem("zeroed"), sem("ctx_clear")
        first_free = sem("first_free")
        max_scored, reduced, max_ready = sem("max_scored"), sem("reduced"), sem("max_ready")
        m_turned, m_taken, m_rest, m_split = sem("m_turned"), sem("m_taken"), sem("m_rest"), sem("m_split")
        m_stored, m_loaded = [sem(f"m_stored{i}") for i in range(2)], [sem(f"m_loaded{i}") for i in range(2)]
        scored, probs_ready, pv_done = sem("scored"), sem("probs_ready"), sem("pv_done")
        ctx_taken, turned, divided, inverted, added = (sem("ctx_taken"), sem("turned"), sem("divided"),
                                                       sem("inverted"), sem("added"))

        def load_group(sp, n, p):
            for stack, parts, side in ((queries[p], qparts, 0), (keys[p], kparts, 1)):
                for r, term in enumerate(TERMS):
                    sp.dma_start(stack[r * D:(r + 1) * D, :, :],
                                 parts[term[side], bass.ds(n * (HG * D), HG * D), :]
                                 .rearrange("(h d) t -> d h t", h=HG)).then_inc(loaded[p], 16)
            sp.dma_start(values[p][:, :, :], vaug[bass.ds(n, 1), :, :].rearrange("g (t p) n -> p (g t) n", p=P)
                         ).then_inc(v_loaded[p], 16)

        def max_half(pe, i, half, k, done):
            p, sc = (k // SC) % 2, k % SC
            t, h = divmod(i, HG)
            if done:
                pe.wait_ge(reduced, 2 * done - 1 + half)
            for c in range(S // 2 // CH):
                k0 = half * (S // 2) + c * CH
                last = nc.tensor.matmul(psA[half][:, c * CH:(c + 1) * CH],
                                        queries[p][0:KROWS, h, sc * CH + t * P:sc * CH + (t + 1) * P],
                                        keys[p][0:KROWS, h, k0:k0 + CH], start=True, stop=True)
            last.then_inc(max_scored, 1)

        def reduce_max(dve, i, done):
            for half in range(2):
                dve.wait_ge(max_scored, 2 * done + half + 1)
                at = i % HG * QT + i // HG
                nc.vector.tensor_reduce(halfmax[:, half, at:at + 1], psA[half][:, :], AX.X, ALU.max,
                                        negate=True).then_inc(reduced, 1)

        def join_max(dve, k, done):
            dve.wait_ge(reduced, (done + 1) * 2 * HG * QT)
            nc.vector.tensor_tensor(negmax[:, k % 2, :], halfmax[:, 0, :], halfmax[:, 1, :],
                                    ALU.min).then_inc(max_ready, 1)
            dve.wait_ge(max_ready, done + 1)

        def turn_max(pe, k):
            nc.tensor.transpose(turned_max, negmax[:, k % 2, :], ident[:, :]).then_inc(m_turned, 1)

        def take_max(act, k, done):
            act.wait_ge(m_turned, done + 1)
            if done:
                act.wait_ge(m_split, done)
            act.activation(mt[:, :], turned_max, ACT.Copy).then_inc(m_taken, 1)
            act.activation(mp[:, k % 2, 0, :], turned_max, ACT.Copy).then_inc(m_taken, 1)

        def split_max(pool, k, done):
            first, second, third = (mp[:, k % 2, a, :] for a in range(3))
            pool.wait_ge(m_taken, 2 * done + 2)
            nc.gpsimd.tensor_tensor(second, mt[:, :], first, ALU.subtract).then_inc(m_rest, 1)
            pool.wait_ge(m_rest, 2 * done + 1)
            nc.gpsimd.tensor_tensor(mt[:, :], mt[:, :], first, ALU.subtract).then_inc(m_rest, 1)
            pool.wait_ge(m_rest, 2 * done + 2)
            nc.gpsimd.tensor_tensor(third, mt[:, :], second, ALU.subtract).then_inc(m_split, 1)

        def place_max(sp, n, k, done):
            sc = k % SC
            uses = 16 * (done // 2 + 1)
            sp.wait_ge(m_split, done + 1)
            sp.dma_start(mparts[bass.ds(n, 1), sc, :, :, :].rearrange("g a r s -> r (g a) s"),
                         mp[:, k % 2, :, :]).then_inc(m_stored[k % 2], 16)
            sp.wait_ge(m_stored[k % 2], uses)
            sp.dma_start(queries[(k // SC) % 2][KROWS:SROWS, :, sc * CH:(sc + 1) * CH],
                         mparts[bass.ds(n, 1), sc, :, :, :].rearrange("g a (h t) s -> (g a) h (t s)", h=HG)
                         ).then_inc(m_loaded[k % 2], 16)
            return uses

        with nc.Block() as block:
            @block.sync
            def _(sp):
                load_group(sp, 0, 0)
                uses = place_max(sp, 0, 0, 0)
                sp.wait_ge(m_loaded[0], uses)
                sp.wait_ge(v_loaded[0], 16)

            @block.gpsimd
            def _(pool):
                for p in range(2):
                    pool.memset(keys[p][KROWS:SROWS, :, :], 1.0).then_inc(ones_set, 1)
                    pool.wait_ge(ones_set, p + 1)
                pool.memset(zeros[:, :], 0.0).then_inc(zero_set, 1)
                pool.wait_ge(zero_set, 1)
                for i in range(8):
                    rows = slice(i * (SLOTS * P // 8), (i + 1) * (SLOTS * P // 8))
                    pool.dma_start(xs[rows, :].rearrange("(p t) e -> p (t e)", p=P), zeros[:, :]).then_inc(zeroed, 16)
                split_max(pool, 0, 0)
                pool.wait_ge(zeroed, 16 * 8)

            @block.tensor
            def _(pe):
                pe.wait_ge(loaded[0], STACK_DMAS)
                for k in range(AHEAD):
                    for i in range(HG * QT):
                        for half in range(2):
                            max_half(pe, i, half, k, k * HG * QT + i)
                    if k == 0:
                        pe.wait_ge(max_ready, 1)
                        turn_max(pe, 0)

            @block.scalar
            def _(act):
                take_max(act, 0, 0)

            @block.vector
            def _(dve):
                nc.vector.memset(psC[:, :], 0.0).then_inc(ctx_clear, 1)
                for k in range(AHEAD):
                    for i in range(HG * QT):
                        reduce_max(dve, i, k * HG * QT + i)
                    join_max(dve, k, k)
                dve.wait_ge(ctx_clear, 1)
        rewind(nc, sems)

        def score(pe, n):
            u, blk = divmod(n, BLOCKS)
            p, sc = u // SC, u % SC
            t, h = divmod(blk, HG)
            if blk == 0 and u:
                pe.wait_ge(m_loaded[u % 2], 16 * ((u + 1) // 2))
            nc.tensor.matmul(psP[n % 2][:, :], keys[p][:, h, t * P:(t + 1) * P],
                             queries[p][:, h, sc * CH:(sc + 1) * CH], start=True, stop=True).then_inc(scored, 1)

        def weigh(pe, quad):
            u, t = divmod(quad, ST)
            p = u // SC
            if t == 0 and u:
                if u == SC:
                    pe.wait_ge(v_loaded[1], 16)
                pe.wait_ge(ctx_taken, u)
            for h in range(HG):
                last = nc.tensor.matmul(psC[32 * h:32 * h + DV, :], values[p][:, t, h * DV:(h + 1) * DV],
                                        probs[:, (quad * HG + h) % RING, :], start=t == 0, stop=t == ST - 1)
            last.then_inc(pv_done, 1)

        def turn(pe, u):
            pe.wait_ge(ctx_taken, u + 1)
            if u:
                pe.wait_ge(m_taken, 2 * (u + 1))
            for t in range(QT):
                last = nc.tensor.transpose(psM[:, t, :, :].rearrange("p h d -> p (h d)"),
                                           ctxT[:, t * P:(t + 1) * P], ident[:, :])
                if t == 0 and u == SC - 1:
                    last.then_inc(first_free, 1)
            last.then_inc(turned, 1)

        def take_ctx(act, u):
            act.wait_ge(pv_done, (u + 1) * ST)
            act.activation(ctxT[:, :], psC[:, :], ACT.Copy).then_inc(ctx_taken, 1)

        def divide(dve, b, gp, u):
            p, sc = u // SC, u % SC
            dve.wait_ge(turned, u + 1)
            nc.vector.reciprocal(rec[:, :, :], psM[:, :, :, D]).then_inc(inverted, 1)
            dve.wait_ge(inverted, u + 1)
            nc.vector.tensor_tensor(part[:, :, :, :], psM[:, :, :, 0:D],
                                    rec[:, :, :].unsqueeze(3).broadcast_to([P, QT, HG, D]),
                                    ALU.mult).then_inc(divided, 1)
            dve.wait_ge(divided, u + 1)
            x_unit = x_sb[:, bass.ds(b * ST + sc * QT, QT), bass.ds((gp * 2 + p) * (HG * D), HG * D)]
            nc.vector.tensor_tensor(x_unit, x_unit, part[:, :, :, :].rearrange("p t h d -> p t (h d)"),
                                    ALU.add).then_inc(added, 1)

        GP = GROUPS // B // 2
        with nc.Fori(0, B) as b, nc.Fori(0, GP) as gp:
            first = (b * GP + gp) * 2
            with nc.Block() as block:
                @block.sync
                def _(sp):
                    load_group(sp, first + 1, 1)
                    for u in range(UNITS):
                        if u == SC:
                            sp.wait_ge(first_free, 1)
                            load_group(sp, (first + 2) & (GROUPS - 1), 0)
                        k = u + 1
                        n = first + k // SC if k < UNITS else (first + 2) & (GROUPS - 1)
                        uses = place_max(sp, n, k, u)
                    sp.wait_ge(m_loaded[UNITS % 2], uses)
                    sp.wait_ge(v_loaded[0], 16)

                @block.gpsimd
                def _(pool):
                    for u in range(UNITS):
                        split_max(pool, u + 1, u)

                @block.tensor
                def _(pe):
                    score(pe, 0)
                    score(pe, 1)
                    for quad in range(UNITS * ST):
                        u, t = divmod(quad, ST)
                        k = u + AHEAD
                        if t == 0 and k % SC == 0:
                            pe.wait_ge(loaded[(k // SC) % 2], STACK_DMAS)
                        for h in range(HG):
                            n = quad * HG + h
                            pe.wait_ge(probs_ready, n + 1)
                            if n + 2 < UNITS * BLOCKS:
                                score(pe, n + 2)
                            if h == 1 and quad:
                                weigh(pe, quad - 1)
                        for half in range(2):
                            max_half(pe, t, half, k, quad)
                        if t == 2 and u:
                            turn(pe, u - 1)
                        if t == 6:
                            if u:
                                pe.wait_ge(divided, u)
                                pe.wait_ge(max_ready, u)
                            turn_max(pe, u + 1)
                    weigh(pe, UNITS * ST - 1)
                    turn(pe, UNITS - 1)

                @block.scalar
                def _(act):
                    for n in range(UNITS * BLOCKS):
                        u, blk = divmod(n, BLOCKS)
                        act.wait_ge(scored, n + 1)
                        if n >= RING and n % HG == 0:
                            act.wait_ge(pv_done, (n - RING) // HG + 1)
                        act.activation(probs[:, n % RING, :], psP[n % 2][:, :], ACT.Exp).then_inc(probs_ready, 1)
                        if u and blk == HG + 1:
                            take_ctx(act, u - 1)
                        if blk == 8 * HG:
                            take_max(act, u + 1, u)
                    take_ctx(act, UNITS - 1)

                @block.vector
                def _(dve):
                    for u in range(UNITS):
                        for i in range(HG * QT):
                            reduce_max(dve, i, u * HG * QT + i)
                            if u and i == 4:
                                divide(dve, b, gp, u - 1)
                        join_max(dve, u + AHEAD, u)
                    divide(dve, b, gp, UNITS - 1)
                    dve.wait_ge(added, UNITS)
            rewind(nc, sems)


def moments(nc, dve, stats, mean, rstd, step, base, ready):
    even, odd = stats[:, :, 1], stats[:, :, 4]
    nc.vector.tensor_tensor(mean[:, :], even, odd, ALU.add).then_inc(step, 1)
    nc.vector.tensor_tensor(rstd[:, :], stats[:, :, 2], stats[:, :, 5], ALU.add).then_inc(step, 1)
    nc.vector.tensor_tensor(stats[:, :, 0], even, odd, ALU.subtract).then_inc(step, 1)
    dve.wait_ge(step, base + 3)
    nc.vector.tensor_scalar(mean[:, :], mean[:, :], 0.5, None, ALU.mult).then_inc(step, 1)
    nc.vector.tensor_scalar(rstd[:, :], rstd[:, :], 1.0 / E, LN_EPS, ALU.mult, ALU.add).then_inc(step, 1)
    nc.vector.tensor_tensor(stats[:, :, 3], stats[:, :, 0], stats[:, :, 0], ALU.mult).then_inc(step, 1)
    dve.wait_ge(step, base + 6)
    nc.vector.scalar_tensor_tensor(rstd[:, :], stats[:, :, 3], 0.25, rstd[:, :], ALU.mult, ALU.add).then_inc(ready, 1)


def route(nc, x_sb, ident, wg, bg, x2d, xs, w1_loaded, w2_sb, w2, w2_loaded, pos, wts, tile_expert):
    with ExitStack() as ctx:
        sb = lambda name, shape, dt=fp32: ctx.enter_context(nc.sbuf_tensor("r_" + name, shape, dt))
        pb = lambda name, shape: ctx.enter_context(nc.psum_tensor("r_" + name, shape, fp32))
        sem = lambda name: ctx.enter_context(nc.semaphore("r_" + name))
        wg_sb, bg_sb = sb("wg_sb", [P, KE, X]), sb("bg_sb", [P, X])
        stats, mean, rstd = sb("stats", [P, NT, 6]), sb("mean", [P, NT]), sb("rstd", [P, NT])
        xn, xnT = sb("xn", [P, 2, E]), sb("xnT", [P, 2, KE, P])
        tri, ones = sb("tri", [P, P], bf16), sb("ones", [P, P], bf16)
        rank = sb("rank", [P, X])
        keep = sb("keep", [P, X, NT])
        slot = sb("slot", [1, SLOTS])
        logits, masked, eq = sb("logits", [P, NT, X]), sb("masked", [P, NT, X]), sb("eq", [P, NT, X])
        hot = [sb(f"hot{k}", [P, NT, X]) for k in range(TOP)]
        best = [sb(f"best{k}", [P, NT]) for k in range(TOP)]
        top, both = sb("top", [P, NT]), sb("both", [P, NT, X], bf16)
        total, upto, place = sb("total", [P, X, NT]), sb("upto", [P, X, NT]), sb("place", [P, NT, X])
        cnt_i, cnt_t = sb("cnt_i", [P, X], i32), sb("cnt_t", [P, X])
        tiles_to, base, one8 = sb("tiles_to", [P, X]), sb("base", [P, X]), sb("one8", [P, X])
        posf, past, texp = sb("posf", [P, NT]), sb("past", [1, SLOTS, X]), sb("texp", [1, SLOTS])
        psT = [pb(f"psT{i}", [P, KE, P]) for i in range(2)]
        psG, psR, psN = pb("psG", [P, NT, X]), pb("psR", [P, NT, X]), pb("psN", [P, NT, X])

        g_loaded, consts, dve_step, stats_ready, std_ready = (sem("g_loaded"), sem("consts"), sem("dve_step"),
                                                              sem("stats_ready"), sem("std_ready"))
        kept, xn_ready, tp_ready, xnT_ready, gated = (sem("kept"), sem("xn_ready"), sem("tp_ready"),
                                                      sem("xnT_ready"), sem("gated"))
        both_ready, ranked, gap_ready, exp_ready, pos_ready, scattered = (sem("both_ready"), sem("ranked"),
            sem("gap_ready"), sem("exp_ready"), sem("pos_ready"), sem("scattered"))
        block = ctx.enter_context(nc.Block())

        @block.sync
        def _(sp):
            sp.dma_start(wg_sb[:, :, :], wg.rearrange("(k p) x -> p k x", p=P)).then_inc(g_loaded, 16)
            sp.dma_start(bg_sb[:, :], bg.rearrange("(a x) -> a x", a=1).broadcast_to([P, X])).then_inc(g_loaded, 16)
            sp.dma_start(x2d.rearrange("(t p) e -> p t e", p=P), x_sb[:, :, :]).then_inc(kept, 16)
            sp.dma_start(w2_sb[:, :, :, :], w2.rearrange("x (k p) d -> p x k d", p=P)).then_inc(w2_loaded, 16)
            sp.wait_ge(kept, 16)

        @block.gpsimd
        def _(pool):
            pool.memset(tri[:, :], 1.0).then_inc(consts, 1)
            pool.memset(ones[:, :], 1.0).then_inc(consts, 1)
            pool.memset(keep[:, :, :], 1.0).then_inc(consts, 1)
            pool.memset(one8[:, :], 1.0).then_inc(consts, 1)
            pool.iota(rank[:, :], pattern=[[-1, X]], base=X, channel_multiplier=0,
                      allow_small_or_imprecise_dtypes=True).then_inc(consts, 1)
            pool.iota(slot[:, :], pattern=[[1, SLOTS]], base=0, channel_multiplier=0,
                      allow_small_or_imprecise_dtypes=True).then_inc(consts, 1)
            pool.wait_ge(consts, 6)
            pool.affine_select(out=tri[:, :], in_=tri[:, :], compare_op=ALU.is_gt, fill=0.0,
                               base=0, pattern=[[1, P]], channel_multiplier=-1).then_inc(consts, 1)
            pool.memset(keep[:, :, 0:1], 0.0).then_inc(consts, 1)
            pool.wait_ge(pos_ready, TOP)
            pool.wait_ge(xn_ready, NT)
            for k in range(TOP):
                for t in range(NT):
                    pool.indirect_dma_start(out=xs, out_offset=bass.IndirectOffsetOnAxis(ap=pos[:, k, t:t + 1], axis=0),
                                            in_=x_sb[:, t, :], in_offset=None).then_inc(scattered, 16)
            pool.wait_ge(scattered, 16 * TOP * NT)

        @block.scalar
        def _(act):
            act.wait_ge(stats_ready, 1)
            act.activation(rstd[:, :], rstd[:, :], ACT.Sqrt).then_inc(std_ready, 1)
            with act.Fori(0, NT // 2) as i:
                for u in range(2):
                    t = 2 * i + u
                    act.wait_ge(tp_ready, t + 1)
                    act.wait_ge(gated, t)
                    act.activation(xnT[:, u, :, :], psT[u][:, :, :], ACT.Copy).then_inc(xnT_ready, 1)
            act.wait_ge(gap_ready, 1)
            act.activation(top[:, :], top[:, :], ACT.Exp).then_inc(exp_ready, 1)

        @block.tensor
        def _(pe):
            pe.wait_ge(g_loaded, 32)
            with pe.Fori(0, NT // 2) as i:
                for u in range(2):
                    t = 2 * i + u
                    pe.wait_ge(xn_ready, t + 1)
                    for k in range(KE):
                        last = nc.tensor.transpose(psT[u][:, k, :], xn[:, u, k * P:(k + 1) * P], ident[:, :])
                    last.then_inc(tp_ready, 1)
                    pe.wait_ge(xnT_ready, t + 1)
                    for k in range(KE):
                        last = nc.tensor.matmul(psG[:, bass.ds(t, 1), :].rearrange("p a x -> p (a x)"), xnT[:, u, k, :],
                                                wg_sb[:, k, :], start=k == 0, stop=k == KE - 1)
                    last.then_inc(gated, 1)
            pe.wait_ge(both_ready, 1)
            pe.wait_ge(consts, 8)
            flat = both[:, :, :].rearrange("p t x -> p (t x)")
            nc.tensor.matmul(psR[:, :, :].rearrange("p t x -> p (t x)"), tri[:, :], flat, start=True, stop=True)
            nc.tensor.matmul(psN[:, :, :].rearrange("p t x -> p (t x)"), ones[:, :], flat,
                             start=True, stop=True).then_inc(ranked, 1)

        @block.vector
        def _(dve):
            with dve.Fori(0, NT) as t:
                nc.vector.bn_stats(stats[:, bass.ds(t, 1), :], x_sb[:, bass.ds(t, 1), :]).then_inc(dve_step, 1)
            dve.wait_ge(dve_step, NT)
            moments(nc, dve, stats, mean, rstd, dve_step, NT, stats_ready)
            dve.wait_ge(std_ready, 1)
            nc.vector.reciprocal(rstd[:, :], rstd[:, :]).then_inc(dve_step, 1)
            dve.wait_ge(dve_step, NT + 7)
            dve.wait_ge(kept, 16)
            with dve.Fori(0, NT // 2) as i:
                for u in range(2):
                    t = 2 * i + u
                    tile = bass.ds(t, 1)
                    dve.wait_ge(tp_ready, t)
                    src = x_sb[:, tile, :].rearrange("p a e -> p (a e)")
                    for dst in (xn[:, u, :], src):
                        last = nc.vector.tensor_scalar(dst, src, mean[:, tile], rstd[:, tile],
                                                       ALU.subtract, ALU.mult)
                    last.then_inc(xn_ready, 1)

            done = [NT + 7]

            def link(ins):
                done[0] += 1
                ins.then_inc(dve_step, 1)
                dve.wait_ge(dve_step, done[0])

            wide = lambda a: a.unsqueeze(2).broadcast_to([P, NT, X])
            each = lambda a: a.unsqueeze(1).broadcast_to([P, NT, X])
            dve.wait_ge(consts, 8)
            dve.wait_ge(gated, NT)
            link(nc.vector.tensor_tensor(logits[:, :, :], psG[:, :, :], each(bg_sb[:, :]), ALU.add))
            src = logits
            for k in range(TOP):
                link(nc.vector.tensor_reduce(best[k][:, :], src[:, :, :], AX.X, ALU.max))
                link(nc.vector.tensor_tensor(eq[:, :, :], src[:, :, :], wide(best[k][:, :]), ALU.is_equal))
                link(nc.vector.tensor_tensor(eq[:, :, :], eq[:, :, :], each(rank[:, :]), ALU.mult))
                link(nc.vector.tensor_reduce(top[:, :], eq[:, :, :], AX.X, ALU.max))
                link(nc.vector.tensor_tensor(hot[k][:, :, :], eq[:, :, :], wide(top[:, :]), ALU.is_equal))
                if k == 0:
                    link(nc.vector.scalar_tensor_tensor(masked[:, :, :], hot[0][:, :, :], -3e38, logits[:, :, :],
                                                        ALU.mult, ALU.add))
                    src = masked
            nc.vector.tensor_tensor(both[:, :, :], hot[0][:, :, :], hot[1][:, :, :], ALU.add).then_inc(both_ready, 1)
            nc.vector.tensor_tensor(top[:, :], best[1][:, :], best[0][:, :], ALU.subtract).then_inc(gap_ready, 1)
            dve.wait_ge(exp_ready, 1)
            link(nc.vector.tensor_scalar(posf[:, :], top[:, :], 1.0, None, ALU.add))
            link(nc.vector.reciprocal(wts[:, 0, :], posf[:, :]))
            link(nc.vector.tensor_tensor(wts[:, 1, :], wts[:, 0, :], top[:, :], ALU.mult))
            dve.wait_ge(ranked, 1)
            link(nc.vector.tensor_copy(total[:, :, :], psN[:, :, :].rearrange("p t x -> p x t")))
            link(nc.vector.tensor_tensor_scan(upto[:, :, :].rearrange("p x t -> p (x t)"),
                                              keep[:, :, :].rearrange("p x t -> p (x t)"),
                                              total[:, :, :].rearrange("p x t -> p (x t)"), 0.0, ALU.mult, ALU.add))
            link(nc.vector.tensor_scalar(cnt_i[:, :], upto[:, :, NT - 1], float(P - 1), None, ALU.add))
            link(nc.vector.tensor_scalar(cnt_i[:, :], cnt_i[:, :], P.bit_length() - 1, None, ALU.arith_shift_right))
            link(nc.vector.tensor_copy(cnt_t[:, :], cnt_i[:, :]))
            link(nc.vector.tensor_tensor_scan(tiles_to[:, :], one8[:, :], cnt_t[:, :], 0.0, ALU.mult, ALU.add))
            link(nc.vector.tensor_tensor(base[:, :], tiles_to[:, :], cnt_t[:, :], ALU.subtract))
            link(nc.vector.tensor_scalar(base[:, :], base[:, :], float(P), None, ALU.mult))
            link(nc.vector.tensor_tensor(upto[:, :, :], upto[:, :, :], total[:, :, :], ALU.subtract))
            link(nc.vector.tensor_tensor(place[:, :, :], psR[:, :, :], upto[:, :, :].rearrange("p x t -> p t x"), ALU.add))
            link(nc.vector.tensor_tensor(place[:, :, :], place[:, :, :], each(base[:, :]), ALU.add))
            for k in range(TOP):
                link(nc.vector.tensor_tensor(eq[:, :, :], place[:, :, :], hot[k][:, :, :], ALU.mult))
                link(nc.vector.tensor_reduce(posf[:, :], eq[:, :, :], AX.X, ALU.add))
                nc.vector.tensor_copy(pos[:, k, :], posf[:, :]).then_inc(pos_ready, 1)
                dve.wait_ge(pos_ready, k + 1)
            link(nc.vector.tensor_tensor(past[:, :, :], tiles_to[0:1, :].unsqueeze(1).broadcast_to([1, SLOTS, X]),
                                         slot[:, :].unsqueeze(2).broadcast_to([1, SLOTS, X]), ALU.is_le))
            link(nc.vector.tensor_reduce(texp[:, :], past[:, :, :], AX.X, ALU.add))
            link(nc.vector.tensor_scalar(texp[:, :], texp[:, :], float(X - 1), None, ALU.min))
            link(nc.vector.tensor_copy(tile_expert[:, :], texp[:, :]))


def experts(nc, ident, w1_sb, w2_sb, b1_sb, b2_sb, b1, b2, w1_loaded, w2_loaded, tile_expert, xs, ys):
    with ExitStack() as ctx:
        sb = lambda name, shape, dt=fp32: ctx.enter_context(nc.sbuf_tensor("e_" + name, shape, dt))
        pb = lambda name, shape: ctx.enter_context(nc.psum_tensor("e_" + name, shape, fp32))
        sem = lambda name: ctx.enter_context(nc.semaphore("e_" + name))
        xt, xT = sb("xt", [P, 2, E]), sb("xT", [P, 2, KE, P])
        h, gT, y = sb("h", [P, F]), sb("gT", [P, 2, KF, P]), sb("y", [P, 2, E])
        psX, psY = pb("psX", [P, KE, P]), pb("psY", [P, E])
        psH, psG = pb("psH", [P, 2, F // 2]), pb("psG", [P, 2, KF // 2, P])
        x_loaded = [sem(f"x_loaded{u}") for u in range(2)]
        y_stored = [sem(f"y_stored{u}") for u in range(2)]
        b_loaded = sem("b_loaded")
        x_turned, x_taken, h_ready, h_taken, g_turned, g_ready, y_ready, y_taken = (
            sem("x_turned"), sem("x_taken"), sem("h_ready"), sem("h_taken"), sem("g_turned"), sem("g_ready"),
            sem("y_ready"), sem("y_taken"))
        block = ctx.enter_context(nc.Block())

        @block.sync
        def _(sp):
            def load(j, u):
                sp.dma_start(xt[:, u, :], xs[bass.ds(j * P, P), :]).then_inc(x_loaded[u], 16)

            sp.dma_start(b1_sb, b1.rearrange("(a x) f -> a x f", a=1).broadcast_to([P, X, F])).then_inc(b_loaded, 16)
            sp.dma_start(b2_sb[:, :, :], b2.rearrange("(a x) f -> a x f", a=1).broadcast_to([P, X, E])).then_inc(b_loaded, 16)
            load(0, 0)
            load(1, 1)
            with sp.Fori(0, SLOTS // 2 - 1) as i:
                for u in range(2):
                    sp.wait_ge(x_turned, 2 * i + u + 1)
                    load(2 * i + 2 + u, u)

        @block.tensor
        def _(pe):
            pe.wait_ge(w1_loaded, 16)

            def expert(j):
                return pe.value_load(tile_expert[0:1, bass.ds(j, 1)], min_val=0, max_val=X - 1)

            def turn_x(j, u, i):
                pe.wait_ge(x_loaded[u], 16 * (i + 1))
                pe.wait_ge(x_taken, j)
                for k in range(KE):
                    last = nc.tensor.transpose(psX[:, k, :], xt[:, u, k * P:(k + 1) * P], ident[:, :])
                last.then_inc(x_turned, 1)

            def up(j, u, e):
                pe.wait_ge(x_taken, j + 1)
                pe.wait_ge(h_taken, 2 * j)
                for c in range(2):
                    for k in range(KE):
                        last = nc.tensor.matmul(psH[:, c, :], xT[:, u, k, :],
                                                w1_sb[:, bass.ds(e, 1), k, c * (F // 2):(c + 1) * (F // 2)]
                                                .rearrange("p a f -> p (a f)"), start=k == 0, stop=k == KE - 1)
                    last.then_inc(h_ready, 1)

            def turn_h(j):
                for c in range(2):
                    pe.wait_ge(h_taken, 2 * j + c + 1)
                    pe.wait_ge(g_ready, 2 * j)
                    for k in range(KF // 2):
                        f = c * (F // 2) + k * P
                        last = nc.tensor.transpose(psG[:, c, k, :], h[:, f:f + P], ident[:, :])
                    last.then_inc(g_turned, 1)

            def down(j, u, e):
                pe.wait_ge(g_ready, 2 * j + 2)
                pe.wait_ge(y_taken, j)
                for k in range(KF):
                    last = nc.tensor.matmul(psY[:, :], gT[:, u, k, :],
                                            w2_sb[:, bass.ds(e, 1), k, :].rearrange("p a f -> p (a f)"),
                                            start=k == 0, stop=k == KF - 1)
                last.then_inc(y_ready, 1)

            turn_x(0, 0, 0)
            up(0, 0, expert(0))
            turn_x(1, 1, 0)
            turn_h(0)
            pe.wait_ge(w2_loaded, 16)
            with pe.Fori(0, SLOTS // 2 - 1) as i:
                for v in range(2):
                    j, u = 2 * i + 1 + v, 1 - v
                    up(j, u, expert(j))
                    turn_x(j + 1, 1 - u, i + 1)
                    down(j - 1, 1 - u, expert(j - 1))
                    turn_h(j)
            up(SLOTS - 1, 1, expert(SLOTS - 1))
            down(SLOTS - 2, 0, expert(SLOTS - 2))
            turn_h(SLOTS - 1)
            down(SLOTS - 1, 1, expert(SLOTS - 1))

        @block.vector
        def _(dve):
            dve.wait_ge(b_loaded, 32)

            def expert(j):
                return dve.value_load(tile_expert[0:1, bass.ds(j, 1)], min_val=0, max_val=X - 1)

            def take_x(j, u):
                dve.wait_ge(x_turned, j + 1)
                nc.vector.tensor_copy(xT[:, u, :, :], psX[:, :, :]).then_inc(x_taken, 1)

            def take_h(j, e):
                for c in range(2):
                    dve.wait_ge(h_ready, 2 * j + c + 1)
                    dve.wait_ge(g_turned, 2 * j)
                    half = slice(c * (F // 2), (c + 1) * (F // 2))
                    nc.vector.tensor_tensor(h[:, half], psH[:, c, :],
                                            b1_sb[:, bass.ds(e, 1), half].rearrange("p a f -> p (a f)"),
                                            ALU.add).then_inc(h_taken, 1)

            def take_y(j, u, i, e):
                dve.wait_ge(y_ready, j + 1)
                dve.wait_ge(y_stored[u], 16 * i)
                nc.vector.tensor_tensor(y[:, u, :], psY[:, :],
                                        b2_sb[:, bass.ds(e, 1), :].rearrange("p a f -> p (a f)"),
                                        ALU.add).then_inc(y_taken, 1)

            take_x(0, 0)
            take_h(0, expert(0))
            take_x(1, 1)
            with dve.Fori(0, SLOTS // 2 - 1) as i:
                for v in range(2):
                    j, u = 2 * i + 1 + v, 1 - v
                    take_h(j, expert(j))
                    take_x(j + 1, 1 - u)
                    take_y(j - 1, 1 - u, i, expert(j - 1))
            take_h(SLOTS - 1, expert(SLOTS - 1))
            take_y(SLOTS - 2, 0, SLOTS // 2 - 1, expert(SLOTS - 2))
            take_y(SLOTS - 1, 1, SLOTS // 2 - 1, expert(SLOTS - 1))

        @block.scalar
        def _(act):
            with act.Fori(0, SLOTS // 2) as i:
                for u in range(2):
                    j = 2 * i + u
                    for c in range(2):
                        act.wait_ge(g_turned, 2 * j + c + 1)
                        act.activation(gT[:, u, c * (KF // 2):(c + 1) * (KF // 2), :], psG[:, c, :, :],
                                       ACT.Gelu).then_inc(g_ready, 1)

        @block.gpsimd
        def _(pool):
            with pool.Fori(0, SLOTS // 2) as i:
                for u in range(2):
                    pool.wait_ge(y_taken, 2 * i + u + 1)
                    pool.dma_start(ys[bass.ds((2 * i + u) * P, P), :], y[:, u, :]).then_inc(y_stored[u], 16)
            for u in range(2):
                pool.wait_ge(y_stored[u], 16 * (SLOTS // 2))


def combine(nc, x2d, ys, pos, wts, out):
    with ExitStack() as ctx:
        sb = lambda name, shape, dt=fp32: ctx.enter_context(nc.sbuf_tensor("c_" + name, shape, dt))
        sem = lambda name: ctx.enter_context(nc.semaphore("c_" + name))
        RING = 4
        xr, yr, r = sb("xr", [P, RING, E]), sb("yr", [P, RING, TOP, E]), sb("r", [P, RING, E])
        x_loaded = [sem(f"x_loaded{i}") for i in range(RING)]
        gathered = [sem(f"gathered{i}") for i in range(RING)]
        stored = [sem(f"stored{i}") for i in range(RING)]
        half, summed = sem("half"), sem("summed")
        block = ctx.enter_context(nc.Block())
        ov = out.rearrange("b s e -> (b s) e")

        @block.gpsimd
        def _(pool):
            for t in range(NT):
                if t >= RING:
                    pool.wait_ge(summed, t - RING + 1)
                for k in range(TOP):
                    pool.indirect_dma_start(out=yr[:, t % RING, k, :], out_offset=None, in_=ys,
                                            in_offset=bass.IndirectOffsetOnAxis(ap=pos[:, k, t:t + 1], axis=0)
                                            ).then_inc(gathered[t % RING], 16)

        @block.scalar
        def _(act):
            for t in range(NT):
                if t >= RING:
                    act.wait_ge(summed, t - RING + 1)
                act.dma_start(xr[:, t % RING, :], x2d[t * P:(t + 1) * P, :]).then_inc(x_loaded[t % RING], 16)

        @block.vector
        def _(dve):
            for t in range(NT):
                i, n = t % RING, t // RING
                dve.wait_ge(x_loaded[i], 16 * (n + 1))
                dve.wait_ge(gathered[i], 32 * (n + 1))
                if n:
                    dve.wait_ge(stored[i], 16 * n)
                nc.vector.scalar_tensor_tensor(r[:, i, :], yr[:, i, 0, :], wts[:, 0, t:t + 1], xr[:, i, :],
                                               ALU.mult, ALU.add).then_inc(half, 1)
                dve.wait_ge(half, t + 1)
                nc.vector.scalar_tensor_tensor(r[:, i, :], yr[:, i, 1, :], wts[:, 1, t:t + 1], r[:, i, :],
                                               ALU.mult, ALU.add).then_inc(summed, 1)

        @block.sync
        def _(sp):
            for t in range(NT):
                sp.wait_ge(summed, t + 1)
                sp.dma_start(ov[t * P:(t + 1) * P, :], r[:, t % RING, :]).then_inc(stored[t % RING], 16)
            for i in range(RING):
                sp.wait_ge(stored[i], 16 * (NT // RING))


_OUT = "out_dram"


def kernel(**inputs):
    import numpy as _np
    import concourse.bacc as _bacc
    from concourse import mybir as _mybir
    from concourse.bass_utils import run_bass_kernel_spmd as _run

    get = {k: _np.asarray(v) for k, v in inputs.items()}
    a, f = "L0_attn_", "L0_ffn_"
    order = [("x", get[a + "hidden_states"])]
    for w in ("q", "k", "v", "s"):
        order.append((f"w{w}T", get[a + "W" + w].T))
        order.append((f"b{w}", get[a + "b" + w]))
    order += [(n.lower(), get[f + n]) for n in ("Wg", "bg", "W1", "b1", "W2", "b2")]
    nc = _bacc.Bacc("TRN2", target_bir_lowering=False, num_devices=1)
    arrays, args = {}, []
    for name, v in order:
        arrays[name] = _np.ascontiguousarray(v)
        args.append(nc.dram_tensor(name, v.shape, _mybir.dt.from_np(v.dtype), kind="ExternalInput").ap())
    args.append(nc.dram_tensor(_OUT, (B, S, E), _mybir.dt.from_np(_np.dtype("float32")), kind="ExternalOutput").ap())
    build(nc, *args)
    return _run(nc, [arrays], core_ids=[0]).results[0][_OUT]
```

```python
import concourse.bass as bass
from concourse import mybir
from contextlib import ExitStack

B, S, E = 2, 2048, 256
H, D = 16, 16
X, F, TOP = 8, 1024, 2
P = 128
N = B * S
NT = N // P
KE, KF = E // P, F // P
CH = 512
HG = 4
DV = D + 1
ST = S // P
SC = S // CH
SLOTS = TOP * N // P + X - 1
LN_EPS = 1e-5
S_MIN, S_RANGE = 0.95, 1.05 - 0.95
QSCALE = D ** -0.5

TERMS = [(0, 0), (0, 1), (0, 2), (1, 0), (1, 1), (2, 0)]
KROWS = len(TERMS) * D
SROWS = KROWS + 3

fp32, bf16 = mybir.dt.float32, mybir.dt.bfloat16
i32 = mybir.dt.int32
ALU = mybir.AluOpType
ACT = mybir.ActivationFunctionType
AX = mybir.AxisListType


def build(nc, x_in, wqT, bq, wkT, bk, wvT, bv, wsT, bs, wg, bg, w1, b1, w2, b2, out):
    scratch = lambda name, shape, dt: nc.dram_tensor(name, shape, dt, kind="Internal").ap()
    qparts = scratch("qparts", [3, B * E, S], bf16)
    kparts = scratch("kparts", [3, B * E, S], bf16)
    mparts = scratch("mparts", [B * H // HG, SC, 3, HG * CH // P, P], bf16)
    vaug = scratch("vaug", [B * H // HG, S, HG * DV], fp32)
    xnd = scratch("xnd", [N, E], fp32)
    yd = scratch("yd", [1 + TOP * N, E], fp32)

    with ExitStack() as ctx:
        sb = lambda name, shape, dt=fp32: ctx.enter_context(nc.sbuf_tensor(name, shape, dt))
        x_sb = sb("x_sb", [P, NT, E])
        w1_sb = sb("w1_sb", [P, X, KE, F])
        ident = sb("ident", [P, P])
        stats = sb("stats", [P, NT, 6])
        w1_loaded = ctx.enter_context(nc.semaphore("w1_loaded"))

        with ExitStack() as early:
            sbe = lambda name, shape, dt: early.enter_context(nc.sbuf_tensor(name, shape, dt))
            stack = (sbe("queries0", [SROWS, HG, S], bf16), sbe("keys0", [SROWS, HG, S], bf16),
                     sbe("values0", [P, ST, HG * DV], fp32))
            project(nc, x_sb, stats, ident, x_in, wqT, bq, wkT, bk, wvT, bv, wsT, bs, qparts, kparts, vaug, stack)
            attend(nc, x_sb, stats, ident, qparts, kparts, mparts, vaug, stack, w1_sb, w1, w1_loaded)
        with ExitStack() as late:
            sbl = lambda name, shape, dt=fp32: late.enter_context(nc.sbuf_tensor(name, shape, dt))
            wts = sbl("wts", [P, TOP, NT])
            with ExitStack() as ffn:
                sbf = lambda name, shape, dt=fp32: ffn.enter_context(nc.sbuf_tensor(name, shape, dt))
                w2_sb = sbf("w2_sb", [P, X, KF, E])
                b1_sb, b2_sb = sbf("b1_sb", [P, X, KF]), sbf("b2_sb", [P, X, E])
                source, target = sbf("source", [P, SLOTS], i32), sbf("target", [P, SLOTS], i32)
                tile_expert = sbf("tile_expert", [1, SLOTS], i32)
                w2_loaded, b_loaded = (ffn.enter_context(nc.semaphore(n)) for n in ("w2_loaded", "b_loaded"))
                route(nc, x_sb, stats, ident, wg, bg, xnd, w2_sb, w2, w2_loaded, b1_sb, b1, b2_sb, b2, b_loaded,
                      wts, source, target, tile_expert)
                experts(nc, ident, w1_sb, w2_sb, b1_sb, b2_sb, w1_loaded, w2_loaded, b_loaded,
                        source, target, tile_expert, xnd, yd)
            combine(nc, x_sb, yd, wts, out)


def project(nc, x_sb, stats, ident, x_in, wqT, bq, wkT, bk, wvT, bv, wsT, bs, qparts, kparts, vaug, stack):
    XQ = 4
    with ExitStack() as ctx:
        sb = lambda name, shape, dt=fp32: ctx.enter_context(nc.sbuf_tensor(name, shape, dt))
        pb = lambda name, shape: ctx.enter_context(nc.psum_tensor(name, shape, fp32))
        sem = lambda name: ctx.enter_context(nc.semaphore(name))
        w_sb = sb("w_sb", [P, 4, KE, E])
        bias = sb("bias", [P, 3, KE])
        bv_sb = sb("bv_sb", [P, E])
        mean = sb("mean", [P, NT])
        rstd = sb("rstd", [P, NT])
        xn = sb("xn", [P, 2, CH // P, E])
        xnT = sb("xnT", [P, 2, KE, CH])
        sig = sb("sig", [P, CH])
        qf = sb("qf", [P, CH])
        kf = sb("kf", [P, CH])
        qp = sb("qp", [P, KE, 3, CH], bf16)
        kp = sb("kp", [P, KE, 3, CH], bf16)
        vsb = sb("vsb", [P, 2, 2, H, DV])
        psT = pb("psT", [P, KE, CH])
        psS, psQ, psK = pb("psS", [P, CH]), pb("psQ", [P, CH]), pb("psK", [P, CH])
        psV = pb("psV", [P, 2, 2, E])

        x_loaded = [sem(f"x_loaded{i}") for i in range(XQ)]
        w_loaded, id_ready = sem("w_loaded"), sem("id_ready")
        dve_step, stats_ready, std_ready = sem("dve_step"), sem("stats_ready"), sem("std_ready")
        xn_ready = sem("xn_ready")
        tp_ready, xnT_ready = sem("tp_ready"), sem("xnT_ready")
        s_ready, q_ready, k_ready, v_ready = sem("s_ready"), sem("q_ready"), sem("k_ready"), sem("v_ready")
        sig_done, q_done, k_done, v_done = sem("sig_done"), sem("q_done"), sem("k_done"), sem("v_done")
        part1, rest1, part2, part3 = sem("part1"), sem("rest1"), sem("part2"), sem("part3")
        gate_step = sem("gate_step")
        parts_stored = [sem(f"parts_stored{j}") for j in range(KE)]
        v_stored = [sem(f"v_stored{i}") for i in range(2)]
        stack_loaded, values_loaded = sem("stack_loaded"), sem("values_loaded")
        block = ctx.enter_context(nc.Block())
        NC = N // CH
        NT0 = NT // XQ
        TC = CH // P

        @block.sync
        def _(sp):
            xv = x_in.rearrange("b (t p) e -> p (b t) e", p=P)
            for i in range(XQ):
                t = slice(i * NT // XQ, (i + 1) * NT // XQ)
                if i == 1:
                    sp.wait_ge(x_loaded[0], 16)
                sp.dma_start(x_sb[:, t, :], xv[:, t, :]).then_inc(x_loaded[i], 16)
            with sp.Fori(0, B) as b:
                with sp.Fori(0, SC) as sc:
                    c = b * SC + sc
                    for j in range(KE):
                        f = bass.ds(b * E + j * P, P)
                        sp.wait_ge(part3, 2 * KE * c + 2 * j + 2)
                        for dst, src in ((qparts, qp), (kparts, kp)):
                            sp.dma_start(dst[:, f, bass.ds(sc * CH, CH)].rearrange("a f t -> f a t"),
                                         src[:, j, :, :]).then_inc(parts_stored[j], 16)
                        sp.wait_ge(v_done, 2 * c + j + 1)
                        for t in range(2):
                            sp.dma_start(vaug[bass.ds(b * (H // HG), H // HG),
                                              bass.ds((sc * TC + 2 * j + t) * P, P), :].rearrange("g p n -> p g n"),
                                         vsb[:, j, t, :, :].rearrange("p (g h) d -> p g (h d)", g=H // HG)
                                         ).then_inc(v_stored[j], 16)
            for j in range(KE):
                sp.wait_ge(parts_stored[j], 32 * NC)
                sp.wait_ge(v_stored[j], 32 * NC)

        @block.gpsimd
        def _(pool):
            pool.memset(ident[:, :], 0.0).then_inc(id_ready, 1)
            pool.wait_ge(id_ready, 1)
            pool.affine_select(out=ident[:, :], in_=ident[:, :], compare_op=ALU.not_equal, fill=1.0,
                               base=0, pattern=[[-1, P]], channel_multiplier=1).then_inc(id_ready, 1)
            for j in range(KE):
                pool.wait_ge(parts_stored[j], 32 * SC)
                pool.wait_ge(v_stored[j], 32 * SC)
            load_group(pool, 0, stack, qparts, kparts, vaug, stack_loaded, values_loaded)
            pool.wait_ge(stack_loaded, 16 * STACK_DMAS)
            pool.wait_ge(values_loaded, 16)

        @block.scalar
        def _(act):
            for i, w in enumerate((wqT, wkT, wsT, wvT)):
                act.dma_start(w_sb[:, i, :, :], w.rearrange("(k p) f -> p k f", p=P)).then_inc(w_loaded, 16)
            for i, b in enumerate((bq, bk, bs)):
                act.dma_start(bias[:, i, :], b.rearrange("(k p) -> p k", p=P), allow_slow_non_contiguous=True).then_inc(w_loaded, 16)
            act.dma_start(bv_sb[:, :], bv.rearrange("(a f) -> a f", a=1).broadcast_to([P, E])).then_inc(w_loaded, 16)
            def deviation(n, tiles):
                act.wait_ge(stats_ready, n)
                act.activation(rstd[:, tiles], rstd[:, tiles], ACT.Sqrt).then_inc(std_ready, 1)

            def take_turned(c, u):
                for k in range(KE):
                    act.wait_ge(tp_ready, KE * c + k + 1)
                    act.activation(xnT[:, u, k, :], psT[:, k, :], ACT.Copy).then_inc(xnT_ready, 1)

            def chunk(c, u, more=True, first=False):
                if first:
                    deviation(2, slice(NT0, NT))
                    act.wait_ge(w_loaded, 16 * 8)
                for j in range(KE):
                    n = KE * c + j
                    act.wait_ge(s_ready, n + 1)
                    if not first or j:
                        act.wait_ge(q_done, n)
                    act.activation(sig[:, :], psS[:, :], ACT.Sigmoid, bias=bias[:, 2, j:j + 1]).then_inc(sig_done, 1)
                    if not first:
                        act.wait_ge(parts_stored[j], 32 * c)
                    act.wait_ge(q_done, n + 1)
                    act.activation(qp[:, j, 0, :], qf[:, :], ACT.Copy).then_inc(part1, 1)
                    act.wait_ge(k_done, n + 1)
                    act.activation(kp[:, j, 0, :], kf[:, :], ACT.Copy).then_inc(part1, 1)
                    if more and j == KE - 1:
                        take_turned(c + 1, 1 - u)
                    act.wait_ge(rest1, 2 * n + 1)
                    act.activation(qp[:, j, 1, :], qf[:, :], ACT.Copy).then_inc(part2, 1)
                    act.wait_ge(rest1, 2 * n + 2)
                    act.activation(kp[:, j, 1, :], kf[:, :], ACT.Copy).then_inc(part2, 1)

            deviation(1, slice(0, NT0))
            take_turned(0, 0)
            chunk(0, 0, first=True)
            chunk(1, 1)
            with act.Fori(1, NC // 2 - 1) as cc:
                for u in range(2):
                    chunk(2 * cc + u, u)
            chunk(NC - 2, 0)
            chunk(NC - 1, 1, more=False)

        @block.tensor
        def _(pe):
            pe.wait_ge(id_ready, 2)

            def turn(c, u):
                pe.wait_ge(xn_ready, c + 1)
                for k in range(KE):
                    for t in range(TC):
                        last = nc.tensor.transpose(psT[:, k, t * P:(t + 1) * P],
                                                   xn[:, u, t, k * P:(k + 1) * P], ident[:, :])
                    last.then_inc(tp_ready, 1)

            def chunk(c, u, more=True, first=False):
                if first:
                    pe.wait_ge(w_loaded, 16 * 8)
                pe.wait_ge(xnT_ready, KE * c + KE)
                for j in range(KE):
                    f = slice(j * P, (j + 1) * P)
                    n = KE * c + j
                    for w, ps, free, ready in ((2, psS, sig_done, s_ready), (0, psQ, q_done, q_ready),
                                               (1, psK, k_done, k_ready)):
                        if not first or j:
                            pe.wait_ge(free, n)
                        for k in range(KE):
                            last = nc.tensor.matmul(ps[:, :], w_sb[:, w, k, f], xnT[:, u, k, :],
                                                    start=k == 0, stop=k == KE - 1)
                        last.then_inc(ready, 1)
                    if more and j == KE - 1:
                        turn(c + 1, 1 - u)
                    if not first:
                        pe.wait_ge(v_done, 2 * c)
                    for t in range(2):
                        tile = slice((2 * j + t) * P, (2 * j + t + 1) * P)
                        for k in range(KE):
                            last = nc.tensor.matmul(psV[:, j, t, :], xnT[:, u, k, tile], w_sb[:, 3, k, :],
                                                    start=k == 0, stop=k == KE - 1)
                    last.then_inc(v_ready, 1)

            turn(0, 0)
            chunk(0, 0, first=True)
            chunk(1, 1)
            with pe.Fori(1, NC // 2 - 1) as cc:
                for u in range(2):
                    chunk(2 * cc + u, u)
            chunk(NC - 2, 0)
            chunk(NC - 1, 1, more=False)

        @block.vector
        def _(dve):
            steps = [0]

            def statistics(parts, tiles, n):
                for i in parts:
                    dve.wait_ge(x_loaded[i], 16)
                    for t in range(i * NT // XQ, (i + 1) * NT // XQ):
                        nc.vector.bn_stats(stats[:, t:t + 1, :], x_sb[:, t:t + 1, :]).then_inc(dve_step, 1)
                        steps[0] += 1
                dve.wait_ge(dve_step, steps[0])
                moments(nc, dve, stats[:, tiles, :], mean[:, tiles], rstd[:, tiles], dve_step, steps[0], stats_ready)
                dve.wait_ge(std_ready, n)
                nc.vector.reciprocal(rstd[:, tiles], rstd[:, tiles]).then_inc(dve_step, 1)
                steps[0] += 7
                dve.wait_ge(dve_step, steps[0])

            def normalise(c, u):
                for t in range(TC):
                    tile = bass.ds(c * TC + t, 1)
                    last = nc.vector.tensor_scalar(xn[:, u, t, :], x_sb[:, tile, :].rearrange("p a e -> p (a e)"),
                                                   mean[:, tile], rstd[:, tile], ALU.subtract, ALU.mult)
                last.then_inc(xn_ready, 1)

            def chunk(c, u, more=True, first=False):
                for j in range(KE):
                    n = KE * c + j
                    dve.wait_ge(sig_done, n + 1)
                    nc.vector.tensor_scalar(sig[:, :], sig[:, :], S_RANGE * QSCALE, S_MIN * QSCALE,
                                            ALU.mult, ALU.add).then_inc(gate_step, 1)
                    dve.wait_ge(gate_step, n + 1)
                    dve.wait_ge(q_ready, n + 1)
                    if not first or j:
                        dve.wait_ge(part3, 2 * n)
                    nc.vector.scalar_tensor_tensor(qf[:, :], psQ[:, :], bias[:, 0, j:j + 1], sig[:, :],
                                                   ALU.add, ALU.mult).then_inc(q_done, 1)
                    dve.wait_ge(k_ready, n + 1)
                    nc.vector.tensor_scalar(kf[:, :], psK[:, :], bias[:, 1, j:j + 1], None,
                                            ALU.add).then_inc(k_done, 1)
                    if j == 0 and more:
                        normalise(c + 1, 1 - u)
                    for f, (rest, parts) in enumerate(((qf, qp), (kf, kp))):
                        dve.wait_ge(part1, 2 * n + f + 1)
                        nc.vector.tensor_tensor(rest[:, :], rest[:, :], parts[:, j, 0, :],
                                                ALU.subtract).then_inc(rest1, 1)
                    for f, (rest, parts) in enumerate(((qf, qp), (kf, kp))):
                        dve.wait_ge(part2, 2 * n + f + 1)
                        nc.vector.tensor_tensor(parts[:, j, 2, :], rest[:, :], parts[:, j, 1, :],
                                                ALU.subtract).then_inc(part3, 1)
                    dve.wait_ge(v_ready, n + 1)
                    if not first:
                        dve.wait_ge(v_stored[j], 32 * c)
                    for t in range(2):
                        last = nc.vector.tensor_tensor(vsb[:, j, t, :, 0:D],
                                                       psV[:, j, t, :].rearrange("p (h d) -> p h d", h=H),
                                                       bv_sb[:, :].rearrange("p (h d) -> p h d", h=H), ALU.add)
                    last.then_inc(v_done, 1)

            statistics(range(1), slice(0, NT0), 1)
            normalise(0, 0)
            dve.wait_ge(w_loaded, 16 * 8)
            nc.vector.memset(vsb[:, :, :, :, D:DV], 1.0)
            statistics(range(1, XQ), slice(NT0, NT), 2)
            chunk(0, 0, first=True)
            chunk(1, 1)
            with dve.Fori(1, NC // 2 - 1) as cc:
                chunk(2 * cc, 0)
                chunk(2 * cc + 1, 1)
            chunk(NC - 2, 0)
            chunk(NC - 1, 1, more=False)


def rewind(nc, sems):
    nc.gpsimd.sem_clear(range(sems[0].num, sems[-1].num + 1))
    nc.all_engine_barrier()


def load_group(engine, n, stack, qparts, kparts, vaug, loaded, v_loaded):
    queries, keys, values = stack
    for rows, parts, side in ((queries, qparts, 0), (keys, kparts, 1)):
        for r, term in enumerate(TERMS):
            engine.dma_start(rows[r * D:(r + 1) * D, :, :],
                             parts[term[side], bass.ds(n * (HG * D), HG * D), :]
                             .rearrange("(h d) t -> d h t", h=HG)).then_inc(loaded, 16)
    engine.dma_start(values[:, :, :], vaug[bass.ds(n, 1), :, :].rearrange("g (t p) n -> p (g t) n", p=P)
                     ).then_inc(v_loaded, 16)


STACK_DMAS = 2 * len(TERMS)


def attend(nc, x_sb, stats, ident, qparts, kparts, mparts, vaug, stack, w1_sb, w1, w1_loaded):
    with ExitStack() as ctx:
        sb = lambda name, shape, dt=fp32: ctx.enter_context(nc.sbuf_tensor("a_" + name, shape, dt))
        pb = lambda name, shape: ctx.enter_context(nc.psum_tensor("a_" + name, shape, fp32))
        UNITS = 2 * SC
        BLOCKS = ST * HG
        RING = 3 * HG
        QT = CH // P
        TILES = HG * QT
        PARTS = S // CH
        BANKS = 3
        LEAD = TILES + 6
        JOINED = ST - 1 - (LEAD - TILES)
        GROUPS = B * H // HG

        queries = [stack[0], sb("queries1", [SROWS, HG, S], bf16)]
        keys = [stack[1], sb("keys1", [SROWS, HG, S], bf16)]
        values = [stack[2], sb("values1", [P, ST, HG * DV])]
        probs = sb("probs", [P, RING, CH])
        ctxT = sb("ctxT", [P, CH])
        rec = sb("rec", [P, QT, HG])
        part = sb("part", [P, QT, HG, D])
        partmax = sb("partmax", [P, TILES, PARTS])
        negmax = sb("negmax", [P, 2, HG * QT])
        mt = sb("mt", [HG * QT, P])
        mp = sb("mp", [HG * QT, 2, 3, P], bf16)
        psA = [pb(f"psA{i}", [P, CH]) for i in range(BANKS)]
        psP = [pb(f"psP{i}", [P, CH]) for i in range(BANKS)]
        psC, psM = pb("psC", [P, CH]), pb("psM", [P, QT, HG, 32])
        turned_max = psM[0:HG * QT, :, :, :].rearrange("p t h d -> p (t h d)")[:, 0:P]

        sems = []

        def sem(name):
            sems.append(ctx.enter_context(nc.semaphore("a_" + name)))
            return sems[-1]

        loaded = [sem(f"stacks_loaded{i}") for i in range(2)]
        v_loaded = [sem(f"values_loaded{i}") for i in range(2)]
        ones_set, ctx_clear = sem("ones_set"), sem("ctx_clear")
        first_free = sem("first_free")
        max_scored, reduced, max_ready = sem("max_scored"), sem("reduced"), sem("max_ready")
        m_turned, m_taken, m_rest, m_split = sem("m_turned"), sem("m_taken"), sem("m_rest"), sem("m_split")
        m_stored, m_loaded = [sem(f"m_stored{i}") for i in range(2)], [sem(f"m_loaded{i}") for i in range(2)]
        scored, probs_ready, pv_done = sem("scored"), sem("probs_ready"), sem("pv_done")
        ctx_taken, turned, divided, inverted, added = (sem("ctx_taken"), sem("turned"), sem("divided"),
                                                       sem("inverted"), sem("added"))

        def load(sp, n, p):
            load_group(sp, n, (queries[p], keys[p], values[p]), qparts, kparts, vaug, loaded[p], v_loaded[p])

        def max_part(pe, i, part, k, done):
            p, sc = (k // SC) % 2, k % SC
            t, h = divmod(i, HG)
            n = done * PARTS + part
            if n >= BANKS:
                pe.wait_ge(reduced, n - BANKS + 1)
            nc.tensor.matmul(psA[n % BANKS][:, :], queries[p][0:KROWS, h, sc * CH + t * P:sc * CH + (t + 1) * P],
                             keys[p][0:KROWS, h, part * CH:(part + 1) * CH], start=True, stop=True
                             ).then_inc(max_scored, 1)

        def reduce_max(dve, i, done):
            for part in range(PARTS):
                n = done * PARTS + part
                dve.wait_ge(max_scored, n + 1)
                at = i % HG * QT + i // HG
                nc.vector.tensor_reduce(partmax[:, at, part:part + 1], psA[n % BANKS][:, :], AX.X, ALU.max,
                                        negate=True).then_inc(reduced, 1)

        def join_max(dve, k, done, tiles):
            dve.wait_ge(reduced, PARTS * tiles)
            nc.vector.tensor_reduce(negmax[:, k % 2, :], partmax[:, :, :], AX.X, ALU.min).then_inc(max_ready, 1)
            dve.wait_ge(max_ready, done + 1)

        def turn_max(pe, k):
            nc.tensor.transpose(turned_max, negmax[:, k % 2, :], ident[:, :]).then_inc(m_turned, 1)

        def take_max(act, k, done):
            act.wait_ge(m_turned, done + 1)
            if done:
                act.wait_ge(m_split, done)
            act.activation(mt[:, :], turned_max, ACT.Copy).then_inc(m_taken, 1)
            act.activation(mp[:, k % 2, 0, :], turned_max, ACT.Copy).then_inc(m_taken, 1)

        def split_max(pool, k, done):
            first, second, third = (mp[:, k % 2, a, :] for a in range(3))
            pool.wait_ge(m_taken, 2 * done + 2)
            nc.gpsimd.tensor_tensor(second, mt[:, :], first, ALU.subtract).then_inc(m_rest, 1)
            pool.wait_ge(m_rest, 2 * done + 1)
            nc.gpsimd.tensor_tensor(mt[:, :], mt[:, :], first, ALU.subtract).then_inc(m_rest, 1)
            pool.wait_ge(m_rest, 2 * done + 2)
            nc.gpsimd.tensor_tensor(third, mt[:, :], second, ALU.subtract).then_inc(m_split, 1)

        def place_max(sp, n, k, done):
            sc = k % SC
            uses = 16 * (done // 2 + 1)
            sp.wait_ge(m_split, done + 1)
            sp.dma_start(mparts[bass.ds(n, 1), sc, :, :, :].rearrange("g a r s -> r (g a) s"),
                         mp[:, k % 2, :, :]).then_inc(m_stored[k % 2], 16)
            sp.wait_ge(m_stored[k % 2], uses)
            sp.dma_start(queries[(k // SC) % 2][KROWS:SROWS, :, sc * CH:(sc + 1) * CH],
                         mparts[bass.ds(n, 1), sc, :, :, :].rearrange("g a (h t) s -> (g a) h (t s)", h=HG)
                         ).then_inc(m_loaded[k % 2], 16)
            return uses

        with nc.Block() as block:
            @block.sync
            def _(sp):
                uses = place_max(sp, 0, 0, 0)
                sp.wait_ge(m_loaded[0], uses)

            @block.gpsimd
            def _(pool):
                for p in range(2):
                    pool.memset(keys[p][KROWS:SROWS, :, :], 1.0).then_inc(ones_set, 1)
                    pool.wait_ge(ones_set, p + 1)
                split_max(pool, 0, 0)

            @block.tensor
            def _(pe):
                for n in range(LEAD):
                    for part in range(PARTS):
                        max_part(pe, n % TILES, part, n // TILES, n)
                    if n == TILES + 2:
                        pe.wait_ge(max_ready, 1)
                        turn_max(pe, 0)

            @block.scalar
            def _(act):
                act.dma_start(w1_sb[:, :, :, :], w1.rearrange("x (k p) f -> p x k f", p=P)).then_inc(w1_loaded, 16)
                take_max(act, 0, 0)

            @block.vector
            def _(dve):
                nc.vector.memset(psC[:, :], 0.0).then_inc(ctx_clear, 1)
                for n in range(LEAD):
                    reduce_max(dve, n % TILES, n)
                    if n == TILES - 1:
                        join_max(dve, 0, 0, n + 1)
                dve.wait_ge(ctx_clear, 1)
        rewind(nc, sems)

        def score(pe, n):
            u, blk = divmod(n, BLOCKS)
            p, sc = u // SC, u % SC
            t, h = divmod(blk, HG)
            if blk == 0 and u:
                pe.wait_ge(m_loaded[u % 2], 16 * ((u + 1) // 2))
            nc.tensor.matmul(psP[n % BANKS][:, :], keys[p][:, h, t * P:(t + 1) * P],
                             queries[p][:, h, sc * CH:(sc + 1) * CH], start=True, stop=True).then_inc(scored, 1)

        def weigh(pe, quad):
            u, t = divmod(quad, ST)
            p = u // SC
            if t == 0 and u:
                if u == SC:
                    pe.wait_ge(v_loaded[1], 16)
                pe.wait_ge(ctx_taken, u)
            pe.wait_ge(probs_ready, (quad + 1) * HG)
            for h in range(HG):
                last = nc.tensor.matmul(psC[32 * h:32 * h + DV, :], values[p][:, t, h * DV:(h + 1) * DV],
                                        probs[:, (quad * HG + h) % RING, :], start=t == 0, stop=t == ST - 1)
            last.then_inc(pv_done, 1)

        def turn(pe, u):
            pe.wait_ge(ctx_taken, u + 1)
            if u:
                pe.wait_ge(m_taken, 2 * (u + 1))
            for t in range(QT):
                last = nc.tensor.transpose(psM[:, t, :, :].rearrange("p h d -> p (h d)"),
                                           ctxT[:, t * P:(t + 1) * P], ident[:, :])
                if t == 0 and u == SC - 1:
                    last.then_inc(first_free, 1)
            last.then_inc(turned, 1)

        def take_ctx(act, u):
            act.wait_ge(pv_done, (u + 1) * ST)
            act.activation(ctxT[:, :], psC[:, :], ACT.Copy).then_inc(ctx_taken, 1)

        def invert(dve, u):
            dve.wait_ge(turned, u + 1)
            nc.vector.reciprocal(rec[:, :, :], psM[:, :, :, D]).then_inc(inverted, 1)

        def divide(dve, u):
            dve.wait_ge(inverted, u + 1)
            nc.vector.tensor_tensor(part[:, :, :, :], psM[:, :, :, 0:D],
                                    rec[:, :, :].unsqueeze(3).broadcast_to([P, QT, HG, D]),
                                    ALU.mult).then_inc(divided, 1)

        def add(dve, b, gp, u):
            p, sc = u // SC, u % SC
            dve.wait_ge(divided, u + 1)
            x_unit = x_sb[:, bass.ds(b * ST + sc * QT, QT), bass.ds((gp * 2 + p) * (HG * D), HG * D)]
            nc.vector.tensor_tensor(x_unit, x_unit, part[:, :, :, :].rearrange("p t h d -> p t (h d)"),
                                    ALU.add).then_inc(added, 1)

        def take_stats(dve, b, u, t):
            tile = bass.ds(b * ST + u % SC * QT + t, 1)
            dve.wait_ge(added, u + 1)
            nc.vector.bn_stats(stats[:, tile, :], x_sb[:, tile, :])

        GP = GROUPS // B // 2
        with nc.Fori(0, B) as b, nc.Fori(0, GP) as gp:
            first = (b * GP + gp) * 2
            with nc.Block() as block:
                @block.sync
                def _(sp):
                    load(sp, first + 1, 1)
                    for u in range(UNITS):
                        if u == SC:
                            sp.wait_ge(first_free, 1)
                            load(sp, (first + 2) & (GROUPS - 1), 0)
                        k = u + 1
                        n = first + k // SC if k < UNITS else (first + 2) & (GROUPS - 1)
                        uses = place_max(sp, n, k, u)
                    sp.wait_ge(m_loaded[UNITS % 2], uses)
                    sp.wait_ge(v_loaded[0], 16)

                @block.gpsimd
                def _(pool):
                    for u in range(UNITS):
                        split_max(pool, u + 1, u)

                @block.tensor
                def _(pe):
                    for n in range(BANKS):
                        score(pe, n)
                    for quad in range(UNITS * ST):
                        u, t = divmod(quad, ST)
                        k, i = divmod(quad + LEAD, TILES)
                        if i == 0 and k % SC == 0:
                            pe.wait_ge(loaded[(k // SC) % 2], 16 * STACK_DMAS)
                        for h in range(HG):
                            n = quad * HG + h
                            if n + BANKS < UNITS * BLOCKS:
                                pe.wait_ge(probs_ready, n + 1)
                                score(pe, n + BANKS)
                            max_part(pe, i, h, k, quad)
                            if h == 1 and quad:
                                weigh(pe, quad - 1)
                        if t == 2 and u:
                            turn(pe, u - 1)
                        if t == JOINED + 1:
                            if u:
                                pe.wait_ge(divided, u)
                            pe.wait_ge(max_ready, u + 1)
                            turn_max(pe, u + 1)
                    weigh(pe, UNITS * ST - 1)
                    turn(pe, UNITS - 1)

                @block.scalar
                def _(act):
                    for n in range(UNITS * BLOCKS):
                        u, blk = divmod(n, BLOCKS)
                        act.wait_ge(scored, n + 1)
                        if n >= RING and n % HG == 0:
                            act.wait_ge(pv_done, (n - RING) // HG + 1)
                        act.activation(probs[:, n % RING, :], psP[n % BANKS][:, :], ACT.Exp).then_inc(probs_ready, 1)
                        if u and blk == HG + 1:
                            take_ctx(act, u - 1)
                        if blk == (JOINED + 2) * HG + 1:
                            take_max(act, u + 1, u)
                    take_ctx(act, UNITS - 1)

                @block.vector
                def _(dve):
                    for quad in range(UNITS * ST):
                        u, t = divmod(quad, ST)
                        k, i = divmod(quad + LEAD, TILES)
                        reduce_max(dve, i, quad)
                        if i == TILES - 1:
                            join_max(dve, k, u, quad + 1)
                        if u and t == 4:
                            invert(dve, u - 1)
                        if u and t == 5:
                            divide(dve, u - 1)
                        if u and t == 6:
                            add(dve, b, gp, u - 1)
                        if u and ST - 2 * QT + 2 <= t < ST - QT + 2:
                            take_stats(dve, b, u - 1, t - (ST - 2 * QT + 2))
                    invert(dve, UNITS - 1)
                    divide(dve, UNITS - 1)
                    add(dve, b, gp, UNITS - 1)
                    for t in range(QT):
                        take_stats(dve, b, UNITS - 1, t)
            rewind(nc, sems)


def moments(nc, dve, stats, mean, rstd, step, base, ready):
    even, odd = stats[:, :, 1], stats[:, :, 4]
    nc.vector.tensor_tensor(mean[:, :], even, odd, ALU.add).then_inc(step, 1)
    nc.vector.tensor_tensor(rstd[:, :], stats[:, :, 2], stats[:, :, 5], ALU.add).then_inc(step, 1)
    nc.vector.tensor_tensor(stats[:, :, 0], even, odd, ALU.subtract).then_inc(step, 1)
    dve.wait_ge(step, base + 3)
    nc.vector.tensor_scalar(mean[:, :], mean[:, :], 0.5, None, ALU.mult).then_inc(step, 1)
    nc.vector.tensor_scalar(rstd[:, :], rstd[:, :], 1.0 / E, LN_EPS, ALU.mult, ALU.add).then_inc(step, 1)
    nc.vector.tensor_tensor(stats[:, :, 3], stats[:, :, 0], stats[:, :, 0], ALU.mult).then_inc(step, 1)
    dve.wait_ge(step, base + 6)
    nc.vector.scalar_tensor_tensor(rstd[:, :], stats[:, :, 3], 0.25, rstd[:, :], ALU.mult, ALU.add).then_inc(ready, 1)


def route(nc, x_sb, stats, ident, wg, bg, xnd, w2_sb, w2, w2_loaded, b1_sb, b1, b2_sb, b2, b_loaded,
          wts, source, target, tile_expert):
    with ExitStack() as ctx:
        sb = lambda name, shape, dt=fp32: ctx.enter_context(nc.sbuf_tensor("r_" + name, shape, dt))
        pb = lambda name, shape: ctx.enter_context(nc.psum_tensor("r_" + name, shape, fp32))
        sem = lambda name: ctx.enter_context(nc.semaphore("r_" + name))
        TC = CH // P
        STEPS = N // CH
        wg_sb, bg_sb = sb("wg_sb", [P, KE, X]), sb("bg_sb", [P, X])
        mean, rstd = sb("mean", [P, NT]), sb("rstd", [P, NT])
        tri, ones = sb("tri", [P, P], bf16), sb("ones", [P, P], bf16)
        rank = sb("rank", [P, X])
        keep = sb("keep", [P, X, NT])
        rows, tiles, slot = sb("rows", [P, P], bf16), sb("tiles", [P, SLOTS], bf16), sb("slot", [1, SLOTS])
        number_p, number_t = sb("number_p", [P, 1]), sb("number_t", [P, TOP, NT], bf16)
        logits, masked, eq = sb("logits", [P, NT, X]), sb("masked", [P, NT, X]), sb("eq", [P, NT, X])
        hot = [sb(f"hot{k}", [P, NT, X]) for k in range(TOP)]
        best = [sb(f"best{k}", [P, NT]) for k in range(TOP)]
        top, both = sb("top", [P, NT]), sb("both", [P, NT, X], bf16)
        total, upto, place = sb("total", [P, X, NT]), sb("upto", [P, X, NT]), sb("place", [P, NT, X])
        cnt_i, cnt_t = sb("cnt_i", [P, X], i32), sb("cnt_t", [P, X])
        tiles_to, base, one8 = sb("tiles_to", [P, X]), sb("base", [P, X]), sb("one8", [P, X])
        past, texp = sb("past", [1, SLOTS, X]), sb("texp", [1, SLOTS])
        pos, tile_i = sb("pos", [P, TOP, NT]), sb("tile_i", [P, TOP, NT], i32)
        pos_tile, in_tile, in_row = sb("pos_tile", [P, TOP, NT]), sb("in_tile", [P, TOP, NT], bf16), sb("in_row", [P, TOP, NT], bf16)
        taken, over = sb("taken", [P, SLOTS]), sb("over", [P, SLOTS])
        psT = [pb(f"psT{i}", [P, KE, CH]) for i in range(2)]
        gateT = sb("gateT", [X, 2, CH])
        with ExitStack() as before:
            xn, xnT = (before.enter_context(nc.sbuf_tensor("r_" + name, [P, 2, n], fp32))
                       for name, n in (("xn", TC * E), ("xnT", KE * CH)))
        row_hot = [sb(f"row_hot{u}", [P, TOP, TC, P], bf16) for u in range(2)]
        tile_hot = [[sb(f"tile_hot{u}{a}", [P, TOP, TC, SLOTS], bf16) for a in range(3)] for u in range(2)]
        psL, psG, psI = pb("psL", [X, CH]), pb("psG", [P, NT, X]), pb("psI", [P, SLOTS])
        psRN = pb("psRN", [P, 2, NT, X])
        psR, psN = psRN[:, 0, :, :], psRN[:, 1, :, :]

        g_loaded, consts, dve_step, stats_ready, std_ready = (sem("g_loaded"), sem("consts"), sem("dve_step"),
                                                              sem("stats_ready"), sem("std_ready"))
        xn_ready, xn_stored, tp_ready, xnT_ready = (sem("xn_ready"), [sem(f"xn_stored{u}") for u in range(2)],
                                                    sem("tp_ready"), sem("xnT_ready"))
        gated, gate_taken, gate_turned = sem("gated"), sem("gate_taken"), sem("gate_turned")
        both_ready, ranked, gap_ready, exp_ready, hot_ready, hot_used = (
            sem("both_ready"), sem("ranked"), sem("gap_ready"), sem("exp_ready"), sem("hot_ready"),
            sem("hot_used"))
        block = ctx.enter_context(nc.Block())

        @block.sync
        def _(sp):
            sp.dma_start(wg_sb[:, :, :], wg.rearrange("(k p) x -> p k x", p=P)).then_inc(g_loaded, 16)
            sp.dma_start(bg_sb[:, :], bg.rearrange("(a x) -> a x", a=1).broadcast_to([P, X])).then_inc(g_loaded, 16)
            with sp.Fori(0, STEPS // 2) as i:
                for u in range(2):
                    sp.wait_ge(xn_ready, 2 * i + u + 1)
                    sp.dma_start(xnd[bass.ds((2 * i + u) * CH, CH), :].rearrange("(t p) e -> p t e", p=P),
                                 xn[:, u, :].rearrange("p (t e) -> p t e", e=E)).then_inc(xn_stored[u], 16)
            sp.dma_start(b1_sb[:, :, :], b1.rearrange("x (k p) -> p x k", p=P), allow_slow_non_contiguous=True).then_inc(b_loaded, 16)
            sp.dma_start(b2_sb[:, :, :], b2.rearrange("(a x) f -> a x f", a=1).broadcast_to([P, X, E])).then_inc(b_loaded, 16)
            sp.dma_start(w2_sb[:, :, :, :], w2.rearrange("x (k p) d -> p x k d", p=P)).then_inc(w2_loaded, 16)
            for u in range(2):
                sp.wait_ge(xn_stored[u], 16 * (STEPS // 2))

        @block.gpsimd
        def _(pool):
            iota = lambda out, pattern, base, step: pool.iota(out, pattern=pattern, base=base, channel_multiplier=step,
                                                              allow_small_or_imprecise_dtypes=True).then_inc(consts, 1)
            pool.memset(tri[:, :], 1.0).then_inc(consts, 1)
            pool.memset(ones[:, :], 1.0).then_inc(consts, 1)
            pool.memset(keep[:, :, :], 1.0).then_inc(consts, 1)
            pool.memset(one8[:, :], 1.0).then_inc(consts, 1)
            iota(rank[:, :], [[-1, X]], X, 0)
            iota(rows[:, :], [[1, P]], 0, 0)
            iota(tiles[:, :], [[1, SLOTS]], 0, 0)
            iota(slot[:, :], [[1, SLOTS]], 0, 0)
            iota(number_p[:, :], [[0, 1]], 1, 1)
            iota(number_t[:, :, :], [[N, TOP], [P, NT]], 0, 0)
            pool.wait_ge(consts, 10)
            pool.affine_select(out=tri[:, :], in_=tri[:, :], compare_op=ALU.is_gt, fill=0.0,
                               base=0, pattern=[[1, P]], channel_multiplier=-1).then_inc(consts, 1)
            pool.memset(keep[:, :, 0:1], 0.0).then_inc(consts, 1)

        @block.scalar
        def _(act):
            act.wait_ge(stats_ready, 1)
            act.activation(rstd[:, :], rstd[:, :], ACT.Sqrt).then_inc(std_ready, 1)

            def take_gate(s):
                act.wait_ge(gated, s + 1)
                if s >= 2:
                    act.wait_ge(gate_turned, s - 1)
                act.activation(gateT[:, s % 2, :], psL[:, :], ACT.Copy).then_inc(gate_taken, 1)

            for s in range(STEPS):
                act.wait_ge(tp_ready, s + 1)
                if s >= 2:
                    act.wait_ge(gated, s - 1)
                for k in range(KE):
                    act.activation(xnT[:, s % 2, k * CH:(k + 1) * CH], psT[s % 2][:, k, :],
                                   ACT.Copy).then_inc(xnT_ready, 1)
                if s:
                    take_gate(s - 1)
            take_gate(STEPS - 1)
            act.wait_ge(gap_ready, 1)
            act.activation(top[:, :], top[:, :], ACT.Exp).then_inc(exp_ready, 1)

        @block.tensor
        def _(pe):
            pe.wait_ge(g_loaded, 32)

            def turn(s, u):
                pe.wait_ge(xn_ready, s + 1)
                for k in range(KE):
                    for t in range(TC):
                        last = nc.tensor.transpose(psT[u][:, k, t * P:(t + 1) * P],
                                                   xn[:, u, t * E + k * P:t * E + (k + 1) * P], ident[:, :])
                last.then_inc(tp_ready, 1)

            def gate(s, u):
                pe.wait_ge(xnT_ready, KE * (s + 1))
                if s:
                    pe.wait_ge(gate_taken, s)
                for k in range(KE):
                    last = nc.tensor.matmul(psL[:, :], wg_sb[:, k, :], xnT[:, u, k * CH:(k + 1) * CH],
                                            start=k == 0, stop=k == KE - 1)
                last.then_inc(gated, 1)

            def turn_gate(s, u):
                pe.wait_ge(gate_taken, s + 1)
                for t in range(TC):
                    last = nc.tensor.transpose(psG[:, s * TC + t, :], gateT[:, u, t * P:(t + 1) * P], ident[0:X, 0:X])
                last.then_inc(gate_turned, 1)

            turn(0, 0)
            for s in range(STEPS):
                if s < STEPS - 1:
                    turn(s + 1, (s + 1) % 2)
                gate(s, s % 2)
                if s:
                    turn_gate(s - 1, (s - 1) % 2)
            turn_gate(STEPS - 1, (STEPS - 1) % 2)
            pe.wait_ge(both_ready, 1)
            pe.wait_ge(consts, 12)
            flat = both[:, :, :].rearrange("p t x -> p (t x)")
            nc.tensor.matmul(psR[:, :, :].rearrange("p t x -> p (t x)"), tri[:, :], flat, start=True, stop=True)
            nc.tensor.matmul(psN[:, :, :].rearrange("p t x -> p (t x)"), ones[:, :], flat,
                             start=True, stop=True).then_inc(ranked, 1)

            def locate(s, u, start, stop):
                pe.wait_ge(hot_ready, s + 1)
                pairs = [(k, t) for k in range(TOP) for t in range(TC)]
                for n, (k, t) in enumerate(pairs):
                    for a in (1, 2):
                        last = nc.tensor.matmul(psI[:, :], row_hot[u][:, k, t, :], tile_hot[u][a][:, k, t, :],
                                                start=start and n == 0 and a == 1,
                                                stop=stop and n == len(pairs) - 1 and a == 2)
                last.then_inc(hot_used, 1)

            for s in range(STEPS):
                locate(s, s % 2, s == 0, s == STEPS - 1)

        @block.vector
        def _(dve):
            moments(nc, dve, stats, mean, rstd, dve_step, 0, stats_ready)
            dve.wait_ge(std_ready, 1)
            nc.vector.reciprocal(rstd[:, :], rstd[:, :]).then_inc(dve_step, 1)
            dve.wait_ge(dve_step, 7)

            for s in range(STEPS):
                u = s % 2
                if s >= 2:
                    dve.wait_ge(tp_ready, s - 1)
                    dve.wait_ge(xn_stored[u], 16 * (s // 2))
                for t in range(TC):
                    n = s * TC + t
                    last = nc.vector.tensor_scalar(xn[:, u, t * E:(t + 1) * E], x_sb[:, n, :],
                                                   mean[:, n:n + 1], rstd[:, n:n + 1], ALU.subtract, ALU.mult)
                last.then_inc(xn_ready, 1)

            done = [7]

            def link(ins):
                done[0] += 1
                ins.then_inc(dve_step, 1)
                dve.wait_ge(dve_step, done[0])

            wide = lambda a: a.unsqueeze(2).broadcast_to([P, NT, X])
            each = lambda a: a.unsqueeze(1).broadcast_to([P, NT, X])
            dve.wait_ge(consts, 12)
            dve.wait_ge(gate_turned, STEPS)
            link(nc.vector.tensor_tensor(logits[:, :, :], psG[:, :, :], each(bg_sb[:, :]), ALU.add))
            src = logits
            for k in range(TOP):
                link(nc.vector.tensor_reduce(best[k][:, :], src[:, :, :], AX.X, ALU.max))
                link(nc.vector.tensor_tensor(eq[:, :, :], src[:, :, :], wide(best[k][:, :]), ALU.is_equal))
                link(nc.vector.tensor_tensor(eq[:, :, :], eq[:, :, :], each(rank[:, :]), ALU.mult))
                link(nc.vector.tensor_reduce(top[:, :], eq[:, :, :], AX.X, ALU.max))
                link(nc.vector.tensor_tensor(hot[k][:, :, :], eq[:, :, :], wide(top[:, :]), ALU.is_equal))
                if k == 0:
                    link(nc.vector.scalar_tensor_tensor(masked[:, :, :], hot[0][:, :, :], -3e38, logits[:, :, :],
                                                        ALU.mult, ALU.add))
                    src = masked
            nc.vector.tensor_tensor(both[:, :, :], hot[0][:, :, :], hot[1][:, :, :], ALU.add).then_inc(both_ready, 1)
            nc.vector.tensor_tensor(top[:, :], best[1][:, :], best[0][:, :], ALU.subtract).then_inc(gap_ready, 1)
            dve.wait_ge(exp_ready, 1)
            link(nc.vector.tensor_scalar(best[0][:, :], top[:, :], 1.0, None, ALU.add))
            link(nc.vector.reciprocal(wts[:, 0, :], best[0][:, :]))
            link(nc.vector.tensor_tensor(wts[:, 1, :], wts[:, 0, :], top[:, :], ALU.mult))
            dve.wait_ge(ranked, 1)
            link(nc.vector.tensor_copy(total[:, :, :], psN[:, :, :].rearrange("p t x -> p x t")))
            link(nc.vector.tensor_tensor_scan(upto[:, :, :].rearrange("p x t -> p (x t)"),
                                              keep[:, :, :].rearrange("p x t -> p (x t)"),
                                              total[:, :, :].rearrange("p x t -> p (x t)"), 0.0, ALU.mult, ALU.add))
            link(nc.vector.tensor_scalar(cnt_i[:, :], upto[:, :, NT - 1], float(P - 1), None, ALU.add))
            link(nc.vector.tensor_scalar(cnt_i[:, :], cnt_i[:, :], P.bit_length() - 1, None, ALU.arith_shift_right))
            link(nc.vector.tensor_copy(cnt_t[:, :], cnt_i[:, :]))
            link(nc.vector.tensor_tensor_scan(tiles_to[:, :], one8[:, :], cnt_t[:, :], 0.0, ALU.mult, ALU.add))
            link(nc.vector.tensor_tensor(base[:, :], tiles_to[:, :], cnt_t[:, :], ALU.subtract))
            link(nc.vector.tensor_scalar(base[:, :], base[:, :], float(P), None, ALU.mult))
            link(nc.vector.tensor_tensor(upto[:, :, :], upto[:, :, :], total[:, :, :], ALU.subtract))
            link(nc.vector.tensor_tensor(place[:, :, :], psR[:, :, :], upto[:, :, :].rearrange("p x t -> p t x"), ALU.add))
            link(nc.vector.tensor_tensor(place[:, :, :], place[:, :, :], each(base[:, :]), ALU.add))
            for k in range(TOP):
                link(nc.vector.tensor_tensor(eq[:, :, :], place[:, :, :], hot[k][:, :, :], ALU.mult))
                link(nc.vector.tensor_reduce(pos[:, k, :], eq[:, :, :], AX.X, ALU.add))
            link(nc.vector.tensor_copy(tile_i[:, :, :], pos[:, :, :]))
            link(nc.vector.tensor_scalar(tile_i[:, :, :], tile_i[:, :, :], P.bit_length() - 1, None, ALU.arith_shift_right))
            link(nc.vector.tensor_copy(pos_tile[:, :, :], tile_i[:, :, :]))
            nc.vector.tensor_copy(in_tile[:, :, :], pos_tile[:, :, :])
            link(nc.vector.scalar_tensor_tensor(in_row[:, :, :], pos_tile[:, :, :], -float(P), pos[:, :, :],
                                                ALU.mult, ALU.add))

            for u in range(2):
                dve.wait_ge(xn_stored[u], 16 * (STEPS // 2))

            def one_hots(s, u):
                if s >= 2:
                    dve.wait_ge(hot_used, s - 1)
                every = lambda a, n: a[:, :].unsqueeze(1).unsqueeze(1).broadcast_to([P, TOP, TC, n])
                spread = lambda a, n: a[:, :, s * TC:(s + 1) * TC].unsqueeze(3).broadcast_to([P, TOP, TC, n])
                is_tile, times_p, times_t = tile_hot[u]
                link(nc.vector.tensor_tensor(is_tile[:, :, :, :], every(tiles, SLOTS), spread(in_tile, SLOTS), ALU.is_equal))
                nc.vector.tensor_tensor(row_hot[u][:, :, :, :], every(rows, P), spread(in_row, P), ALU.is_equal)
                nc.vector.tensor_scalar(times_p[:, :, :, :], is_tile[:, :, :, :], number_p[:, :], None, ALU.mult)
                nc.vector.tensor_tensor(times_t[:, :, :, :], is_tile[:, :, :, :], spread(number_t, SLOTS),
                                        ALU.mult).then_inc(hot_ready, 1)

            for s in range(STEPS):
                one_hots(s, s % 2)
            link(nc.vector.tensor_tensor(past[:, :, :], tiles_to[0:1, :].unsqueeze(1).broadcast_to([1, SLOTS, X]),
                                         slot[:, :].unsqueeze(2).broadcast_to([1, SLOTS, X]), ALU.is_le))
            link(nc.vector.tensor_reduce(texp[:, :], past[:, :, :], AX.X, ALU.add))
            link(nc.vector.tensor_scalar(texp[:, :], texp[:, :], float(X - 1), None, ALU.min))
            link(nc.vector.tensor_copy(tile_expert[:, :], texp[:, :]))
            dve.wait_ge(hot_used, STEPS)
            nc.vector.tensor_copy(target[:, :], psI[:, :])
            link(nc.vector.tensor_scalar(taken[:, :], psI[:, :], -1.0, 0.0, ALU.add, ALU.max))
            link(nc.vector.tensor_scalar(over[:, :], taken[:, :], float(N), float(N), ALU.is_ge, ALU.mult))
            nc.vector.tensor_tensor(source[:, :], taken[:, :], over[:, :], ALU.subtract)


def experts(nc, ident, w1_sb, w2_sb, b1_sb, b2_sb, w1_loaded, w2_loaded, b_loaded, source, target, tile_expert, xnd, yd):
    with ExitStack() as ctx:
        sb = lambda name, shape, dt=fp32: ctx.enter_context(nc.sbuf_tensor("e_" + name, shape, dt))
        pb = lambda name, shape: ctx.enter_context(nc.psum_tensor("e_" + name, shape, fp32))
        sem = lambda name: ctx.enter_context(nc.semaphore("e_" + name))
        RING = 4
        HALF = KF // 2
        xt, xT = sb("xt", [P, RING, E]), sb("xT", [P, 2, KE, P])
        w1_cur, b1_cur = [sb(f"w1_cur{u}", [P, KE, F]) for u in range(2)], [sb(f"b1_cur{u}", [P, KF]) for u in range(2)]
        gT, y = sb("gT", [P, 2, KF, P]), sb("y", [P, 2, E])
        psX, psY, psH = pb("psX", [P, KE, P]), pb("psY", [P, E]), pb("psH", [P, KF, P])
        x_loaded = [sem(f"x_loaded{r}") for r in range(RING)]
        y_stored = sem("y_stored")
        x_turned, x_taken, w_copied, h_ready, g_ready, y_ready, y_taken = (
            sem("x_turned"), sem("x_taken"), sem("w_copied"), sem("h_ready"), sem("g_ready"), sem("y_ready"),
            sem("y_taken"))
        block = ctx.enter_context(nc.Block())

        LAST = (SLOTS - 1) // RING * RING

        @block.gpsimd
        def _(pool):
            def gather(j):
                if j >= RING:
                    pool.wait_ge(x_turned, j - RING + 1)
                pool.indirect_dma_start(out=xt[:, j % RING, :], out_offset=None, in_=xnd,
                                        in_offset=bass.IndirectOffsetOnAxis(ap=source[:, j:j + 1], axis=0)
                                        ).then_inc(x_loaded[j % RING], 16)

            for j in range(RING):
                gather(j)
            for j in range(SLOTS):
                if j:
                    pool.wait_ge(y_stored, 16 * j)
                pool.wait_ge(y_taken, j + 1)
                pool.indirect_dma_start(out=yd, out_offset=bass.IndirectOffsetOnAxis(ap=target[:, j:j + 1], axis=0),
                                        in_=y[:, j % 2, :], in_offset=None).then_inc(y_stored, 16)
                if j + RING < SLOTS:
                    gather(j + RING)
            pool.wait_ge(y_stored, 16 * SLOTS)

        @block.tensor
        def _(pe):
            def turn_x(j, v, i):
                pe.wait_ge(x_loaded[v], 16 * (i + 1))
                if not (isinstance(j, int) and j == 0):
                    pe.wait_ge(x_taken, j)
                for k in range(KE):
                    last = nc.tensor.transpose(psX[:, k, :], xt[:, v, k * P:(k + 1) * P], ident[:, :])
                last.then_inc(x_turned, 1)

            def up(j, v):
                u = v % 2
                pe.wait_ge(x_taken, j + 1)
                pe.wait_ge(w_copied, 2 * j + 2)
                for c in range(2):
                    if not (isinstance(j, int) and j == 0):
                        pe.wait_ge(g_ready, 2 * j - 1 + c)
                    for f in range(c * HALF, (c + 1) * HALF):
                        for k in range(KE):
                            last = nc.tensor.matmul(psH[:, f, :], w1_cur[u][:, k, f * P:(f + 1) * P], xT[:, u, k, :],
                                                    start=k == 0, stop=k == KE - 1)
                    last.then_inc(h_ready, 1)

            def down(j, v):
                u = v % 2
                e = pe.value_load(tile_expert[0:1, bass.ds(j, 1)], min_val=0, max_val=X - 1)
                pe.wait_ge(g_ready, 2 * j + 2)
                if not (isinstance(j, int) and j == 0):
                    pe.wait_ge(y_taken, j)
                for k in range(KF):
                    last = nc.tensor.matmul(psY[:, :], gT[:, u, k, :],
                                            w2_sb[:, bass.ds(e, 1), k, :].rearrange("p a f -> p (a f)"),
                                            start=k == 0, stop=k == KF - 1)
                last.then_inc(y_ready, 1)

            turn_x(0, 0, 0)
            for j in range(RING):
                up(j, j)
                turn_x(j + 1, (j + 1) % RING, (j + 1) // RING)
                if j == 0:
                    pe.wait_ge(w2_loaded, 16)
                else:
                    down(j - 1, j - 1)
            with pe.Fori(1, LAST // RING) as i:
                for v in range(RING):
                    j = RING * i + v
                    up(j, v)
                    turn_x(j + 1, (v + 1) % RING, i + (v + 1) // RING)
                    down(j - 1, v - 1)
            for j in range(LAST, SLOTS):
                up(j, j % RING)
                if j < SLOTS - 1:
                    turn_x(j + 1, (j + 1) % RING, (j + 1) // RING)
                down(j - 1, (j - 1) % RING)
            down(SLOTS - 1, (SLOTS - 1) % RING)

        @block.vector
        def _(dve):
            def expert(j):
                return dve.value_load(tile_expert[0:1, bass.ds(j, 1)], min_val=0, max_val=X - 1)

            def copy_w(j, v):
                u, fresh = v % 2, isinstance(j, int) and j < 2
                e = expert(j)
                if not fresh:
                    dve.wait_ge(h_ready, 2 * j - 2)
                nc.vector.tensor_scalar(w1_cur[u][:, :, :], w1_sb[:, bass.ds(e, 1), :, :].rearrange("p a k f -> p (a k) f"),
                                        1.0, None, ALU.mult).then_inc(w_copied, 1)
                if not fresh:
                    dve.wait_ge(g_ready, 2 * j - 2)
                nc.vector.tensor_scalar(b1_cur[u][:, :], b1_sb[:, bass.ds(e, 1), :].rearrange("p a f -> p (a f)"),
                                        1.0, None, ALU.mult).then_inc(w_copied, 1)

            def take_x(j, v):
                dve.wait_ge(x_turned, j + 1)
                nc.vector.tensor_copy(xT[:, v % 2, :, :], psX[:, :, :]).then_inc(x_taken, 1)

            def take_y(j, v):
                e = expert(j)
                dve.wait_ge(y_ready, j + 1)
                if not (isinstance(j, int) and j < 2):
                    dve.wait_ge(y_stored, 16 * j - 16)
                nc.vector.tensor_tensor(y[:, v % 2, :], psY[:, :],
                                        b2_sb[:, bass.ds(e, 1), :].rearrange("p a f -> p (a f)"),
                                        ALU.add).then_inc(y_taken, 1)

            dve.wait_ge(w1_loaded, 16)
            dve.wait_ge(b_loaded, 32)
            copy_w(0, 0)
            take_x(0, 0)
            for j in range(RING):
                copy_w(j + 1, j + 1)
                take_x(j + 1, j + 1)
                if j:
                    take_y(j - 1, j - 1)
            with dve.Fori(1, LAST // RING) as i:
                for v in range(RING):
                    j = RING * i + v
                    copy_w(j + 1, v + 1)
                    take_x(j + 1, v + 1)
                    take_y(j - 1, v - 1)
            for j in range(LAST, SLOTS):
                if j < SLOTS - 1:
                    copy_w(j + 1, j + 1)
                    take_x(j + 1, j + 1)
                take_y(j - 1, j - 1)
            take_y(SLOTS - 1, SLOTS - 1)

        @block.scalar
        def _(act):
            def gelu(j, u):
                for c in range(2):
                    act.wait_ge(h_ready, 2 * j + c + 1)
                    for f in range(c * HALF, (c + 1) * HALF):
                        last = act.activation(gT[:, u, f, :], psH[:, f, :], ACT.Gelu, bias=b1_cur[u][:, f:f + 1])
                    last.then_inc(g_ready, 1)

            with act.Fori(0, SLOTS // 2) as i:
                for u in range(2):
                    gelu(2 * i + u, u)
            for j in range(SLOTS // 2 * 2, SLOTS):
                gelu(j, j % 2)


def combine(nc, x_sb, yd, wts, out):
    with ExitStack() as ctx:
        sem = lambda name: ctx.enter_context(nc.semaphore("c_" + name))
        TC, STEPS = CH // P, N // CH
        yr = [ctx.enter_context(nc.sbuf_tensor(f"c_yr{r}", [P, TOP, TC, E], fp32)) for r in range(4)]
        RING = len(yr)
        loaded = [sem(f"loaded{r}") for r in range(RING)]
        half, summed, stored = sem("half"), sem("summed"), sem("stored")
        block = ctx.enter_context(nc.Block())
        ov = out.rearrange("b (t p) e -> p (b t) e", p=P)

        @block.sync
        def _(sp):
            for s in range(STEPS):
                if s >= RING:
                    sp.wait_ge(summed, s - RING + 1)
                for k in range(TOP):
                    first = 1 + k * N + s * CH
                    sp.dma_start(yr[s % RING][:, k, :, :], yd[first:first + CH, :].rearrange("(t p) e -> p t e", p=P)
                                 ).then_inc(loaded[s % RING], 16)

        @block.vector
        def _(dve):
            for s in range(STEPS):
                dve.wait_ge(loaded[s % RING], 32 * (s // RING + 1))
                for k, ready in enumerate((half, summed)):
                    if k:
                        dve.wait_ge(half, s + 1)
                    for t in range(TC):
                        n = s * TC + t
                        last = nc.vector.scalar_tensor_tensor(x_sb[:, n, :], yr[s % RING][:, k, t, :], wts[:, k, n:n + 1],
                                                              x_sb[:, n, :], ALU.mult, ALU.add)
                    last.then_inc(ready, 1)

        @block.scalar
        def _(act):
            for s in range(STEPS):
                act.wait_ge(summed, s + 1)
                act.dma_start(ov[:, s * TC:(s + 1) * TC, :], x_sb[:, s * TC:(s + 1) * TC, :]).then_inc(stored, 16)
            act.wait_ge(stored, 16 * STEPS)


_OUT = "out_dram"


def kernel(**inputs):
    import numpy as _np
    import concourse.bacc as _bacc
    from concourse import mybir as _mybir
    from concourse.bass_utils import run_bass_kernel_spmd as _run

    get = {k: _np.asarray(v) for k, v in inputs.items()}
    a, f = "L0_attn_", "L0_ffn_"
    order = [("x", get[a + "hidden_states"])]
    for w in ("q", "k", "v", "s"):
        order.append((f"w{w}T", get[a + "W" + w].T))
        order.append((f"b{w}", get[a + "b" + w]))
    order += [(n.lower(), get[f + n]) for n in ("Wg", "bg", "W1", "b1", "W2", "b2")]
    nc = _bacc.Bacc("TRN2", target_bir_lowering=False, num_devices=1)
    arrays, args = {}, []
    for name, v in order:
        arrays[name] = _np.ascontiguousarray(v)
        args.append(nc.dram_tensor(name, v.shape, _mybir.dt.from_np(v.dtype), kind="ExternalInput").ap())
    args.append(nc.dram_tensor(_OUT, (B, S, E), _mybir.dt.from_np(_np.dtype("float32")), kind="ExternalOutput").ap())
    build(nc, *args)
    return _run(nc, [arrays], core_ids=[0]).results[0][_OUT]
```
